# Optimizing a Trainium2 kernel written in Bass

```python
import numpy as np
import jax
import jax.numpy as jnp

def _softmax(x, axis=-1):
    return jax.nn.softmax(x, axis=axis)

def _gelu(x):
    return jax.nn.gelu(x, approximate=True)

def _silu(x):
    return jax.nn.silu(x)

def _sigmoid(x):
    return jax.nn.sigmoid(x)

def _layernorm(x, axis=-1, eps=1e-05):
    m = jnp.mean(x, axis=axis, keepdims=True)
    v = jnp.var(x, axis=axis, keepdims=True)
    return (x - m) / jnp.sqrt(v + eps)

def _scatter_add(tgt, idx, src, axis=0):
    return tgt.at[idx].add(src)

def _segment_sum(src, seg, n):
    return jax.ops.segment_sum(src, seg, n)
kernel_name = 'mk_gnn_preln_d2_gnn_r32_651906'

def setup_inputs(seed: int=0):
    np.random.seed(seed)
    _w = jnp.asarray

    def _rec_inputs():
        import jax
        import jax.numpy as jnp
        _gk = jax.random.key(seed)
        x = -0.0003713 + 1 * jax.random.normal(jax.random.fold_in(_gk, 1), (3125, 128), jnp.float32)
        src = jax.random.randint(jax.random.fold_in(_gk, 2), (50000,), 0, 3125, jnp.int32)
        dst = jax.random.randint(jax.random.fold_in(_gk, 3), (50000,), 0, 3125, jnp.int32)
        _o = jnp.argsort(dst, stable=True)
        src = src[_o]
        dst = dst[_o]
        edge_type_16 = jax.random.randint(jax.random.fold_in(_gk, 13), (50000,), 0, 16, jnp.int32)
        return (x, src, dst, edge_type_16)
    x, src, dst, edge_type_16 = _rec_inputs()

    def _L0_gnn_setup():
        import jax, jax.numpy as jnp
        import numpy as np
        N_NODES = 3125
        N_EDGES = 50000
        D = 128
        key = jax.random.key(seed)
        ks = jax.random.split(key, 6)
        feat = jax.random.normal(ks[0], (N_NODES, D), dtype=jnp.float32)
        src = jax.random.randint(ks[1], (N_EDGES,), 0, N_NODES, dtype=jnp.int32)
        dst = jax.random.randint(ks[2], (N_EDGES,), 0, N_NODES, dtype=jnp.int32)
        eps = jnp.zeros((1,), dtype=jnp.float32)
        scale = 1.0 / np.sqrt(D)
        W1 = jax.random.normal(ks[3], (D, D), dtype=jnp.float32) * scale
        b1 = jnp.zeros((D,), dtype=jnp.float32)
        W2 = jax.random.normal(ks[4], (D, D), dtype=jnp.float32) * scale
        b2 = jnp.zeros((D,), dtype=jnp.float32)
        return {'feat': feat, 'src': src, 'dst': dst, 'eps': eps, 'W1': W1, 'b1': b1, 'W2': W2, 'b2': b2}
    _L0_gnn_all = _L0_gnn_setup()
    _L0_gnn_in = {k: v for k, v in _L0_gnn_all.items() if k in ('eps', 'W1', 'b1', 'W2', 'b2')}
    del _L0_gnn_all

    def _L1_gnn_setup():
        import jax, jax.numpy as jnp
        import numpy as np
        N_NODES = 3125
        N_EDGES = 18750
        D_IN = 128
        D_OUT = 128
        N_REL = 16
        N_BASES = 8
        key = jax.random.key(seed)
        ks = jax.random.split(key, 6)
        x = jax.random.normal(ks[0], (N_NODES, D_IN), dtype=jnp.float32)
        edge_index = jax.random.randint(ks[1], (2, N_EDGES), 0, N_NODES, dtype=jnp.int64)
        edge_type = jax.random.randint(ks[2], (N_EDGES,), 0, N_REL, dtype=jnp.int64)
        b_lim = float(np.sqrt(6.0 / (D_IN + D_OUT)))
        c_lim = float(np.sqrt(6.0 / (N_REL + N_BASES)))
        w_lim = float(np.sqrt(6.0 / (D_IN + D_OUT)))
        bases = jax.random.uniform(ks[3], (N_BASES, D_IN, D_OUT), jnp.float32, -b_lim, b_lim)
        coefficients = jax.random.uniform(ks[4], (N_REL, N_BASES), jnp.float32, -c_lim, c_lim)
        w_self = jax.random.uniform(ks[5], (D_OUT, D_IN), jnp.float32, -w_lim, w_lim)
        return {'x': x, 'edge_index': edge_index, 'edge_type': edge_type, 'bases': bases, 'coefficients': coefficients, 'w_self': w_self}
    _L1_gnn_all = _L1_gnn_setup()
    _L1_gnn_in = {k: v for k, v in _L1_gnn_all.items() if k in ('bases', 'coefficients', 'w_self')}
    del _L1_gnn_all
    return {'x': x, 'src': src, 'dst': dst, 'edge_type_16': edge_type_16, 'L0_gnn_eps': _L0_gnn_in['eps'], 'L0_gnn_W1': _L0_gnn_in['W1'], 'L0_gnn_b1': _L0_gnn_in['b1'], 'L0_gnn_W2': _L0_gnn_in['W2'], 'L0_gnn_b2': _L0_gnn_in['b2'], 'L1_gnn_bases': _L1_gnn_in['bases'], 'L1_gnn_coefficients': _L1_gnn_in['coefficients'], 'L1_gnn_w_self': _L1_gnn_in['w_self']}

def reference(x, src, dst, edge_type_16, L0_gnn_eps, L0_gnn_W1, L0_gnn_b1, L0_gnn_W2, L0_gnn_b2, L1_gnn_bases, L1_gnn_coefficients, L1_gnn_w_self):
    import jax
    import jax.numpy as jnp

    def _L0_gnn_ref(feat, src, dst, eps, W1, b1, W2, b2):
        import jax, jax.numpy as jnp
        import numpy as np
        N_NODES = 3125
        N_EDGES = 50000
        D = 128
        msgs = feat[src]
        neigh = jax.ops.segment_sum(msgs, dst, num_segments=N_NODES)
        rst = (1.0 + eps[0]) * feat + neigh
        h = jax.nn.relu(rst @ W1 + b1)
        h = h @ W2 + b2
        return jax.nn.relu(h)

    def _L1_gnn_ref(x, edge_index, edge_type, bases, coefficients, w_self):
        import jax, jax.numpy as jnp
        import numpy as np
        N_NODES = 3125
        N_EDGES = 18750
        D_IN = 128
        D_OUT = 128
        N_REL = 16
        N_BASES = 8
        out = x @ w_self.T
        weights = jnp.einsum('rb,bio->rio', coefficients, bases)
        row, col = (edge_index[0], edge_index[1])
        xc = x[col]
        n_rel = weights.shape[0]
        msg = jnp.zeros((xc.shape[0], w_self.shape[0]), dtype=x.dtype)
        for r in range(n_rel):
            sel = (edge_type == r)[:, None]
            msg = msg + jnp.where(sel, xc @ weights[r], jnp.zeros((), x.dtype))
        out = out.at[row].add(msg)
        return out
    edge_index = jnp.stack([src, dst])
    h = jnp.maximum(_layernorm(x, axis=-1), 0.0)
    x = x + _L0_gnn_ref(h, src, dst, L0_gnn_eps, L0_gnn_W1, L0_gnn_b1, L0_gnn_W2, L0_gnn_b2)
    h = jnp.maximum(_layernorm(x, axis=-1), 0.0)
    x = x + _L1_gnn_ref(h, edge_index, edge_type_16, L1_gnn_bases, L1_gnn_coefficients, L1_gnn_w_self)
    return x

_drawn_inputs = setup_inputs


def setup_inputs(seed=0):
    import zlib

    import numpy as np

    out = dict(_drawn_inputs(seed))
    spreads = {'L0_gnn_b1': (0.0, 0.595), 'L0_gnn_b2': (0.0, 0.413)}
    factors = {}
    for name, (base, spread) in spreads.items():
        noise = np.random.default_rng([zlib.crc32(name.encode()), seed]).standard_normal(out[name].shape)
        drawn = base * np.exp(spread * noise) if base else spread * noise
        out[name] = jnp.asarray(drawn.astype(out[name].dtype))
    for name, factor in factors.items():
        out[name] = (out[name] * factor).astype(out[name].dtype)
    return out
```

```python
import numpy as np
import concourse.bass as bass
from concourse import mybir
from contextlib import ExitStack

F32 = mybir.dt.float32
F16 = mybir.dt.float16
BF16 = mybir.dt.bfloat16
I32 = mybir.dt.int32
ALU = mybir.AluOpType
ACT = mybir.ActivationFunctionType
AX = mybir.AxisListType

N_NODES, N_EDGES, D, N_REL, N_BASES = 3125, 50000, 128, 16, 8
P = 128

TILES = 25
NP = N_NODES // TILES
DIV_MUL, DIV_SHIFT = 5243, 17

EC = 400
EP = N_EDGES // EC

CHUNKS = (N_EDGES + TILES * (P - 1)) // P
GROUP, GROUPS = 13, 4
RING = GROUP * GROUPS
HOTS = 2 * GROUP
ROUNDS = -(-CHUNKS // RING)
CHP = ROUNDS * RING
GROW = 16
SORT_PER_ROUND = EC // ROUNDS
SORT_IN_GROUP = [SORT_PER_ROUND * (g + 1) // GROUPS - SORT_PER_ROUND * g // GROUPS for g in range(GROUPS)]
SORT_BUFS = 5
BIG = 1000.0

BANK = 512
BT = BANK // D
NBANK = -(-TILES // BT)
SPLIT = 112
EPS = 1e-5


def build(nc, x, src, dst, etype, eps, W1, b1, W2, b2, bases, coef, w_self, out):
    ctx = ExitStack()
    with ctx:
        def sb(name, shape, dt):
            return ctx.enter_context(nc.sbuf_tensor(name, shape, dt))

        def sem(name):
            return ctx.enter_context(nc.semaphore(name))

        h_table = nc.dram_tensor("h_table", [N_NODES, D], F32).ap()
        z_table = nc.dram_tensor("z_table", [N_NODES * N_REL, D], F32).ap()

        iota_i = sb("iota_i", [P, BANK], I32)
        pidx_i = sb("pidx_i", [P, 4], I32)
        iota_f = sb("iota_f", [P, BANK], F32)
        iota_h = sb("iota_h", [P, BANK], F16)
        pidx = sb("pidx", [P, 4], F32)
        ident = sb("ident", [P, P], F32)
        before = sb("before", [P, P], F32)
        ones = sb("ones", [P, P], F32)
        zeros_h = sb("zeros_h", [P, P], F16)
        w1_sb = sb("w1_sb", [D, D], F32)
        w2_sb = sb("w2_sb", [D, D], F32)
        ws_sb = sb("ws_sb", [D, D], F32)
        wsT = sb("wsT", [D, D], F32)
        b1_sb = sb("b1_sb", [D, 1], F32)
        b2_sb = sb("b2_sb", [1, D], F32)
        eps1 = sb("eps1", [P, 1], F32)
        coef_sb = sb("coef_sb", [P, N_REL * N_BASES], F32)
        bases_sb = sb("bases_sb", [D, N_BASES, D], F32)
        w_rel = sb("w_rel", [D, N_REL, D], F32)
        ends_i = [sb("dst_i", [EP, EC], I32), sb("src_i", [EP, EC], I32)]
        dst_i, src_i = ends_i
        type_i = sb("type_i", [EP, EC], I32)
        t0 = sb("t0", [EP, EC], I32)
        t1 = sb("t1", [EP, EC], I32)
        low_i = sb("low_i", [EP, EC], I32)
        tile_h = sb("tile_h", [EP, EC], F16)
        row_i = sb("row_i", [EP, EC], I32)
        member = sb("member", [EP, TILES, EC], BF16)
        spare = sb("spare", [P, TILES * EC], F32)
        running = spare[0:EP, :].rearrange("p (b c) -> p b c", c=EC)
        pos_i = sb("pos_i", [EP, EC], I32)
        chunk_f = [sb(f"chunk_f{l}", [EP, EC], F32) for l in range(2)]
        place_f = [sb(f"place_f{l}", [EP, EC], F32) for l in range(2)]
        code_a = [sb(f"code_a{l}", [EP, EC], F32) for l in range(2)]
        code_b = [sb(f"code_b{l}", [EP, EC], F32) for l in range(2)]
        count = sb("count", [EP, TILES], F32)
        lower = sb("lower", [EP, TILES], F32)
        adjust = sb("adjust", [EP, TILES], F32)
        need_i = sb("need_i", [P, TILES], I32)
        need_f = sb("need_f", [P, TILES], F32)
        upto = sb("upto", [P, TILES], F32)
        le_scr = sb("le_scr", [P, TILES], F32)
        tile_of = sb("tile_of", [P, 4], F32)
        tile_off = [sb(f"tile_off{l}", [1, ROUNDS * GROUPS, GROW], I32) for l in range(2)]
        chunk_hot = sb("chunk_hot", [EP, SORT_BUFS, CHP], F16)
        place_val = sb("place_val", [EP, SORT_BUFS, 2, P], F16)
        s0 = sb("s0", [P, CHP], I32)
        s1 = sb("s1", [P, CHP], I32)
        s2 = sb("s2", [P, CHP], I32)
        pad_f = sb("pad_f", [P, CHP], F32)
        row_of = [sb(f"row_of{l}", [P, CHP], I32) for l in range(2)]
        key_of = [sb(f"key_of{l}", [P, CHP], F32) for l in range(2)]
        row_stage = sb("row_stage", [P, GROUPS, GROUP], I32)
        gathered = sb("gathered", [P, RING, D], F32)
        node_hot = sb("node_hot", [P, HOTS, NP], F32)
        x_sb = sb("x_sb", [NP, TILES, D], F32)
        h_sb = sb("h_sb", [NP, TILES, D], F32)
        stats = sb("stats", [NP, TILES, 6], F32)
        mv = sb("mv", [NP, TILES, 2], F32)
        sd = sb("sd", [NP, TILES], F32)
        rstd = sb("rstd", [NP, TILES], F32)
        epsc = sb("epsc", [P, 1], F32)
        flat = spare[0:EP, :]
        z_stage = spare[0:NP, 0:4 * 1024].rearrange("p (s n) -> p s n", s=4)
        h2T = spare[:, 4096:4096 + TILES * NP]
        featT = spare[:, 7400:8400].rearrange("p (s n) -> p s n", s=2)
        hidT = spare[:, 8400:9400].rearrange("p (s n) -> p s n", s=2)

        ps = ctx.enter_context(nc.psum_tensor("ps", [P, 8, BANK], F32))
        psf = ps[:, :, :].rearrange("p b c -> p (b c)")
        LASTB = NBANK - 1
        USED = (TILES - BT * LASTB) * D
        pre_ps = ps[0:EP, 7, 448:448 + TILES]
        tot_ps = ps[:, 7, 480:480 + TILES]
        cut = BANK - USED
        sort_regions = [
            [(0, 0, CHP, ps[:, 7, 0:CHP]), (1, 0, CHP, ps[:, 0, 0:CHP])],
            [(0, 0, CHP, ps[:, 7, 0:CHP]), (1, 0, cut, ps[:, LASTB, USED:BANK]),
             (1, cut, CHP, ps[:, 7, CHP:CHP + CHP - cut])],
        ]

        ld_edge, ld_x, ld_w, ld_c = sem("ld_edge"), sem("ld_x"), sem("ld_w"), sem("ld_c")
        iota_done = sem("iota_done")
        consts_done = sem("consts_done")
        v = sem("v")
        a = sem("a")
        count_ready = sem("count_ready")
        prefix_done = sem("prefix_done")
        tileof_ready = sem("tileof_ready")
        tilerow_done = sem("tilerow_done")
        toff_ready = sem("toff_ready")
        hot_ready = sem("hot_ready")
        hot_used = sem("hot_used")
        decoded = sem("decoded")
        staged = sem("staged")
        begun = sem("begun")
        got = [[sem(f"got{l}_{g}") for g in range(GROUPS)] for l in range(2)]
        nhot_ready = sem("nhot_ready")
        nhot_used = sem("nhot_used")
        var_ready = sem("var_ready")
        sd_ready = sem("sd_ready")
        norm_ready = sem("norm_ready")
        h_ready = sem("h_ready")
        h_stored = sem("h_stored")
        rst_ready = sem("rst_ready")
        featT_ps = sem("featT_ps")
        featT_ready = sem("featT_ready")
        hid_ps = sem("hid_ps")
        hid_ready = sem("hid_ready")
        y_ps = sem("y_ps")
        y_used = sem("y_used")
        h2T_ps = sem("h2T_ps")
        h2T_ready = sem("h2T_ready")
        wsT_ps = sem("wsT_ps")
        wsT_ready = sem("wsT_ready")
        wrel_ready = sem("wrel_ready")
        z_ps = sem("z_ps")
        z_even, z_odd = sem("z_even"), sem("z_odd")
        z_stored = [sem(f"z_stored{s}") for s in range(4)]
        self_ps = sem("self_ps")
        self_used = sem("self_used")
        out_ready = sem("out_ready")
        out_stored = sem("out_stored")

        x_rows = x.rearrange("(p t) d -> p t d", t=TILES)
        h_rows = h_table.rearrange("(p t) d -> p t d", t=TILES)
        z_rows = z_table.rearrange("(p t r) d -> p t (r d)", t=TILES, r=N_REL)
        out_rows = out.rearrange("(p t) d -> p t d", t=TILES)
        PARTS = ((0, SPLIT), (SPLIT, NP))
        groups = [(BT * g, min(TILES, BT * (g + 1))) for g in range(NBANK)]

        block = ctx.enter_context(nc.Block())

        @block.sync
        def _(sp):
            for t, d in ((dst_i, dst), (src_i, src), (type_i, etype)):
                sp.dma_start(t[:, :], d.rearrange("(p c) -> p c", c=EC)).then_inc(ld_edge, 16)
            for p0, p1 in PARTS:
                sp.dma_start(x_sb[p0:p1, :, :], x_rows[p0:p1, :, :]).then_inc(ld_x, 16)
            sp.dma_start(w1_sb[:, :], W1).then_inc(ld_w, 16)
            sp.dma_start(w2_sb[:, :], W2).then_inc(ld_w, 16)
            sp.dma_start(ws_sb[:, :], w_self).then_inc(ld_w, 16)
            sp.dma_start(b1_sb[:, :], b1.rearrange("(p o) -> p o", o=1)).then_inc(ld_w, 16)
            sp.dma_start(b2_sb[:, :], b2.rearrange("(o d) -> o d", o=1)).then_inc(ld_w, 16)
            sp.dma_start(eps1[:, :], eps.rearrange("(o d) -> o d", o=1).to_broadcast([P, 1])).then_inc(ld_w, 16)
            sp.dma_start(coef_sb[:, :], coef.rearrange("(o r) b -> o (r b)", o=1).to_broadcast([P, N_REL * N_BASES])).then_inc(ld_c, 16)
            sp.dma_start(bases_sb[:, :, :], bases.rearrange("b i o -> i b o")).then_inc(ld_c, 16)
            sp.wait_ge(h_ready, 1)
            for p0, p1 in PARTS:
                sp.dma_start(h_rows[p0:p1, :, :], h_sb[p0:p1, :, :]).then_inc(h_stored, 16)
            for t in range(TILES):
                for half in range(2):
                    slot = (2 * t + half) % 4
                    if half == 0:
                        sp.wait_ge(z_even, t + 1)
                    else:
                        sp.wait_ge(z_odd, t + 1)
                    for p0, p1 in PARTS:
                        sp.dma_start(z_rows[p0:p1, t, half * 1024:(half + 1) * 1024],
                                     z_stage[p0:p1, slot, :]).then_inc(z_stored[slot], 16)
            for g in range(NBANK):
                sp.wait_ge(out_ready, g + 1)
                a0, a1 = groups[g]
                for p0, p1 in PARTS:
                    sp.dma_start(out_rows[p0:p1, a0:a1, :], x_sb[p0:p1, a0:a1, :]).then_inc(out_stored, 16)
            sp.wait_ge(out_stored, 32 * NBANK)

        @block.gpsimd
        def _(pool):
            pool.iota(iota_i[:, :], [[1, BANK]], base=0, channel_multiplier=0).then_inc(iota_done, 1)
            pool.iota(pidx_i[:, :], [[P, 4]], base=0, channel_multiplier=1).then_inc(iota_done, 1)
            for l in range(2):
                table = (h_table, z_table)[l]
                if l == 1:
                    for q in range(3):
                        pool.wait_ge(z_stored[q], 32 * ((2 * TILES - q + 3) // 4))
                with nc.gpsimd.Fori(0, ROUNDS) as r:
                    for g in range(GROUPS):
                        if l == 0:
                            pool.wait_ge(h_stored, 32)
                        else:
                            pool.wait_ge(z_stored[3], 32 * ((2 * TILES - 3 + 3) // 4))
                        pool.wait_ge(staged, r * GROUPS + (l * ROUNDS * GROUPS + g + 1))
                        pool.sem_inc(begun, 1)
                        for i in range(GROUP):
                            pool.indirect_dma_start(
                                gathered[:, g * GROUP + i, :], None, table,
                                bass.IndirectOffsetOnAxis(ap=row_stage[:, g, i:i + 1], axis=0)).then_inc(got[l][g], 16)

        @block.scalar
        def _(act):
            done = 0

            def own(ins):
                nonlocal done
                ins.then_inc(a, 1)
                done += 1
                act.wait_ge(a, done)

            act.wait_ge(consts_done, 1)
            act.wait_ge(var_ready, 1)
            nc.scalar.activation(sd[:, :], mv[:, :, 1], ACT.Sqrt, bias=epsc[0:NP, :]).then_inc(sd_ready, 1)
            act.wait_ge(norm_ready, 1)
            nc.scalar.activation(h_sb[:, :, :], h_sb[:, :, :], ACT.Relu).then_inc(h_ready, 1)

            def stage_rows(l):
                act.wait_ge(decoded, l + 1)
                with nc.scalar.Fori(0, ROUNDS) as r:
                    for g in range(GROUPS):
                        act.wait_ge(nhot_used, r * RING + (l * CHP + (g + 1) * GROUP))
                        nc.scalar.copy(row_stage[:, g, :], row_of[l][:, bass.ds(r * RING + g * GROUP, GROUP)]).then_inc(staged, 1)

            stage_rows(0)
            for g, (a0, a1) in enumerate(groups):
                w = (a1 - a0) * NP
                act.wait_ge(featT_ps, g + 1)
                nc.scalar.copy(featT[:, g % 2, 0:w], ps[:, g % 2, 0:w]).then_inc(featT_ready, 1)
                act.wait_ge(hid_ps, g + 1)
                nc.scalar.activation(hidT[:, g % 2, 0:w], ps[:, 2 + g % 2, 0:w], ACT.Relu, bias=b1_sb[:, :]).then_inc(hid_ready, 1)
            act.wait_ge(var_ready, 2)
            nc.scalar.activation(sd[:, :], mv[:, :, 1], ACT.Sqrt, bias=epsc[0:NP, :]).then_inc(sd_ready, 1)
            act.wait_ge(norm_ready, 2)
            nc.scalar.activation(h_sb[:, :, :], h_sb[:, :, :], ACT.Relu).then_inc(h_ready, 1)
            for g, (a0, a1) in enumerate(groups):
                act.wait_ge(h2T_ps, g + 1)
                nc.scalar.copy(h2T[:, a0 * NP:a1 * NP], ps[:, g % 2, 0:(a1 - a0) * NP]).then_inc(h2T_ready, 1)
            for t in range(TILES):
                n = 2 * t + 1
                act.wait_ge(z_ps, n + 1)
                if n >= 4:
                    act.wait_ge(z_stored[n % 4], 32 * (n // 4))
                nc.scalar.copy(z_stage[:, n % 4, :], psf[0:NP, (n % 4) * 1024:(n % 4 + 1) * 1024]).then_inc(z_odd, 1)
            stage_rows(1)

        @block.vector
        def _(dve):
            done = 0

            def own(ins):
                nonlocal done
                ins.then_inc(v, 1)
                done += 1
                dve.wait_ge(v, done)

            V = nc.vector
            dve.wait_ge(iota_done, 2)
            V.tensor_copy(iota_f[:, :], iota_i[:, :])
            V.tensor_copy(iota_h[:, :], iota_i[:, :])
            V.memset(ones[:, :], 1.0)
            V.memset(zeros_h[:, :], 0.0)
            V.memset(epsc[:, :], EPS)
            own(V.tensor_copy(pidx[:, :], pidx_i[:, :]))
            V.tensor_scalar(ident[:, :], iota_f[:, 0:P], pidx[:, 0:1], None, ALU.is_equal)
            V.tensor_scalar(before[:, :], iota_f[:, 0:P], pidx[:, 0:1], None, ALU.is_gt).then_inc(consts_done, 1)

            def layer_norm(stage):
                own(V.bn_aggr(mv[:, 0, :], stats[:, 0, :]))
                for t in range(1, TILES):
                    last = V.bn_aggr(mv[:, t, :], stats[:, t, :])
                last.then_inc(var_ready, 1)
                dve.wait_ge(var_ready, stage + 1)
                dve.wait_ge(sd_ready, stage + 1)
                own(V.reciprocal(rstd[:, :], sd[:, :]))
                for t in range(TILES):
                    last = V.tensor_scalar(h_sb[:, t, :], x_sb[:, t, :], mv[:, t, 0:1], rstd[:, t:t + 1],
                                           ALU.subtract, ALU.mult)
                last.then_inc(norm_ready, 1)

            dve.wait_ge(ld_x, 32)
            for t in range(TILES):
                last = V.bn_stats(stats[:, t, :], x_sb[:, t, :])
            own(last)
            layer_norm(0)

            dve.wait_ge(ld_edge, 48)

            def rank(l):
                key = ends_i[l]
                if l == 1:
                    own(V.scalar_tensor_tensor(row_i[:, :], dst_i[:, :], float(N_REL), type_i[:, :], ALU.mult, ALU.add))
                row = src_i if l == 0 else row_i
                own(V.tensor_scalar(t0[:, :], key[:, :], float(DIV_MUL), None, ALU.mult))
                own(V.tensor_scalar(low_i[:, :], t0[:, :], DIV_SHIFT, None, ALU.logical_shift_right))
                own(V.scalar_tensor_tensor(tile_h[:, :], low_i[:, :], -float(TILES), key[:, :], ALU.mult, ALU.add))
                for b in range(TILES):
                    last = V.tensor_scalar(member[:, b, :], tile_h[:, :], float(b), None, ALU.is_equal)
                own(last)
                mflat = member[:, :, :].rearrange("p b c -> p (b c)")
                own(V.tensor_tensor_scan(flat, mflat, mflat, 0.0, ALU.add, ALU.bypass))
                V.tensor_copy(count[:, 0:1], running[:, 0, EC - 1:EC])
                V.tensor_tensor(count[:, 1:TILES], running[:, 1:TILES, EC - 1], running[:, 0:TILES - 1, EC - 1],
                                ALU.subtract).then_inc(count_ready, 1)
                dve.wait_ge(prefix_done, l + 1)
                dve.wait_ge(count_ready, l + 1)
                V.tensor_copy(lower[:, :], pre_ps)
                own(V.tensor_scalar(need_i[:, :], tot_ps, float(P - 1), None, ALU.add))
                own(V.tensor_scalar(need_i[:, :], need_i[:, :], 7, None, ALU.logical_shift_right))
                own(V.tensor_copy(need_f[:, :], need_i[:, :]))
                own(V.tensor_tensor_scan(upto[:, :], need_f[:, :], need_f[:, :], 0.0, ALU.add, ALU.bypass))
                for q in range(4):
                    last = V.tensor_scalar(le_scr[:, :], upto[:, :], pidx[:, q:q + 1], 0.0, ALU.is_le, ALU.add,
                                           accum_out=tile_of[:, q:q + 1])
                    own(last)
                V.tensor_scalar(tile_of[:, :], tile_of[:, :], float(TILES - 1), float(D), ALU.min, ALU.mult).then_inc(tileof_ready, 1)
                own(V.tensor_tensor(need_f[:, :], upto[:, :], need_f[:, :], ALU.subtract))
                own(V.scalar_tensor_tensor(adjust[:, :], need_f[0:EP, :], float(P), lower[:, :], ALU.mult, ALU.add))
                own(V.scalar_tensor_tensor(adjust[:, :], adjust[:, :], -1.0, count[:, :], ALU.add, ALU.add))
                own(V.tensor_tensor(adjust[:, :], adjust[:, :], running[:, :, EC - 1], ALU.subtract))
                for b in range(TILES):
                    last = V.scalar_tensor_tensor(running[:, b, :], running[:, b, :], adjust[:, b:b + 1], member[:, b, :],
                                                  ALU.add, ALU.mult)
                own(last)
                own(V.tensor_reduce(chunk_f[l][:, :], running[:, :, :].rearrange("p b c -> p c b"), AX.X, ALU.add))
                own(V.tensor_copy(pos_i[:, :], chunk_f[l][:, :]))
                V.tensor_scalar(t0[:, :], pos_i[:, :], 7, None, ALU.logical_shift_right)
                own(V.tensor_scalar(t1[:, :], pos_i[:, :], P - 1, None, ALU.bitwise_and))
                V.tensor_copy(chunk_f[l][:, :], t0[:, :])
                own(V.tensor_copy(place_f[l][:, :], t1[:, :]))
                V.tensor_scalar(t0[:, :], row[:, :], 8, 3, ALU.logical_shift_right, ALU.logical_shift_left)
                own(V.tensor_scalar(t1[:, :], low_i[:, :], 4, None, ALU.logical_shift_right))
                own(V.scalar_tensor_tensor(code_a[l][:, :], t0[:, :], 1.0, t1[:, :], ALU.add, ALU.add))
                V.tensor_scalar(t0[:, :], row[:, :], 255, 4, ALU.bitwise_and, ALU.logical_shift_left)
                own(V.tensor_scalar(t1[:, :], low_i[:, :], 15, None, ALU.bitwise_and))
                own(V.scalar_tensor_tensor(code_b[l][:, :], t0[:, :], -2048.0, t1[:, :], ALU.add, ALU.add))
                dve.wait_ge(tilerow_done, l + 1)
                V.tensor_copy(tile_off[l][:, :, 0:GROUP], ps[0:1, 7, 0:CHP].rearrange("p (g i) -> p g i", i=GROUP)).then_inc(toff_ready, 1)

            def sort_column(l, col, n, nth):
                s = nth % SORT_BUFS
                dve.wait_ge(hot_used, n)
                V.tensor_scalar(chunk_hot[:, s, :], iota_h[0:EP, 0:CHP], chunk_f[l][:, bass.ds(col, 1)], None, ALU.is_equal)
                for k, code in enumerate((code_a, code_b)):
                    last = V.tensor_scalar(place_val[:, s, k, :], iota_h[0:EP, 0:P], place_f[l][:, bass.ds(col, 1)],
                                           code[l][:, bass.ds(col, 1)], ALU.is_equal, ALU.mult)
                last.then_inc(hot_ready, 1)

            def decode(l):
                dve.wait_ge(hot_used, SORT_BUFS + EC * (l + 1))
                pa = ps[:, 7, 0:CHP]
                own(V.tensor_scalar(s0[:, :], pa, -1.0, 0.0, ALU.add, ALU.max))
                V.tensor_scalar(pad_f[:, :], pa, 0.0, BIG, ALU.is_equal, ALU.mult)
                for k, c0, c1, where in sort_regions[l]:
                    if k == 1:
                        last = V.tensor_scalar(s1[:, c0:c1], where, 2048.0, None, ALU.add)
                own(last)
                own(V.tensor_scalar(s2[:, :], s0[:, :], 3, 8, ALU.logical_shift_right, ALU.logical_shift_left))
                own(V.tensor_scalar(row_of[l][:, :], s1[:, :], 4, None, ALU.logical_shift_right))
                V.tensor_tensor(row_of[l][:, :], row_of[l][:, :], s2[:, :], ALU.add).then_inc(decoded, 1)
                dve.wait_ge(decoded, l + 1)
                own(V.tensor_scalar(s0[:, :], s0[:, :], 7, 4, ALU.bitwise_and, ALU.logical_shift_left))
                own(V.tensor_scalar(s1[:, :], s1[:, :], 15, None, ALU.bitwise_and))
                own(V.tensor_tensor(pad_f[:, :], pad_f[:, :], s0[:, :], ALU.add))
                own(V.tensor_tensor(key_of[l][:, :], pad_f[:, :], s1[:, :], ALU.add))

            def node_hots(l, sorting):
                with nc.vector.Fori(0, ROUNDS) as r:
                    col = 0
                    for g in range(GROUPS):
                        dve.wait_ge(nhot_used, r * RING + (l * CHP + (g + 1) * GROUP + RING - HOTS))
                        for i in range(GROUP):
                            V.tensor_scalar(node_hot[:, (g * GROUP + i) % HOTS, :], iota_f[:, 0:NP],
                                            key_of[l][:, bass.ds(r * RING + (g * GROUP + i), 1)],
                                            None, ALU.is_equal).then_inc(nhot_ready, 1)
                        if sorting:
                            for _ in range(SORT_IN_GROUP[g]):
                                sort_column(1, r * SORT_PER_ROUND + col, r * SORT_PER_ROUND + (EC + col + 1), col)
                                col += 1

            rank(0)
            with nc.vector.Fori(0, EC // SORT_BUFS) as r:
                for c in range(SORT_BUFS):
                    sort_column(0, r * SORT_BUFS + c, r * SORT_BUFS + (c + 1), c)
            decode(0)
            rank(1)
            node_hots(0, True)
            decode(1)

            dve.wait_ge(ld_c, 32)
            with nc.vector.Fori(0, N_REL) as r:
                pass_ = V.tensor_scalar(w_rel[:, bass.ds(r, 1), :], bases_sb[:, 0:1, :], coef_sb[:, bass.ds(r * N_BASES, 1)],
                                        None, ALU.mult)
                pass_.then_inc(wrel_ready, 1)
                for b in range(1, N_BASES):
                    dve.wait_ge(wrel_ready, r * N_BASES + b)
                    V.scalar_tensor_tensor(w_rel[:, bass.ds(r, 1), :], bases_sb[:, b:b + 1, :],
                                           coef_sb[:, bass.ds(r * N_BASES + b, 1)], w_rel[:, bass.ds(r, 1), :],
                                           ALU.mult, ALU.add).then_inc(wrel_ready, 1)
            dve.wait_ge(wsT_ps, 1)
            V.tensor_copy(wsT[:, :], ps[:, 7, 0:D]).then_inc(wsT_ready, 1)

            dve.wait_ge(ld_w, 96)
            own(V.tensor_scalar(eps1[:, :], eps1[:, :], 1.0, None, ALU.add))
            dve.wait_ge(nhot_used, RING + CHP)
            for g, (a0, a1) in enumerate(groups):
                V.scalar_tensor_tensor(h_sb[:, a0:a1, :], h_sb[:, a0:a1, :], eps1[0:NP, :],
                                       psf[0:NP, a0 * D:a1 * D].rearrange("p (t d) -> p t d", d=D),
                                       ALU.mult, ALU.add).then_inc(rst_ready, 1)
            for g, (a0, a1) in enumerate(groups):
                dve.wait_ge(y_ps, g + 1)
                own(V.scalar_tensor_tensor(x_sb[:, a0:a1, :],
                                           ps[0:NP, 4 + g % 2, 0:(a1 - a0) * D].rearrange("p (t d) -> p t d", d=D),
                                           0.0, x_sb[:, a0:a1, :], ALU.max, ALU.add))
                for t in range(a0, a1):
                    last = V.bn_stats(stats[:, t, :], x_sb[:, t, :])
                last.then_inc(y_used, 1)
                dve.wait_ge(y_used, g + 1)
            layer_norm(1)
            for t in range(TILES):
                n = 2 * t
                dve.wait_ge(z_ps, n + 1)
                if n >= 4:
                    dve.wait_ge(z_stored[n % 4], 32 * (n // 4))
                V.tensor_copy(z_stage[:, n % 4, :], psf[0:NP, (n % 4) * 1024:(n % 4 + 1) * 1024]).then_inc(z_even, 1)
            for g, (a0, a1) in enumerate(groups):
                dve.wait_ge(self_ps, g + 1)
                V.tensor_tensor(x_sb[:, a0:a1, :], x_sb[:, a0:a1, :],
                                ps[0:NP, g, 0:(a1 - a0) * D].rearrange("p (t d) -> p t d", d=D), ALU.add).then_inc(self_used, 1)
            dve.wait_ge(self_used, NBANK)
            node_hots(1, False)
            dve.wait_ge(nhot_used, RING + 2 * CHP)
            for g, (a0, a1) in enumerate(groups):
                V.tensor_tensor(x_sb[:, a0:a1, :], x_sb[:, a0:a1, :],
                                psf[0:NP, a0 * D:a1 * D].rearrange("p (t d) -> p t d", d=D), ALU.add).then_inc(out_ready, 1)

        @block.tensor
        def _(pe):
            T = nc.tensor
            pe.sem_inc(nhot_used, RING)
            pe.sem_inc(hot_used, SORT_BUFS)
            pe.wait_ge(consts_done, 1)

            def zero_bank(b):
                return T.matmul(ps[:, b, :], zeros_h[:, :], iota_h[:, :], start=True, stop=False, skip_group_check=True)

            def rank_sums(l):
                pe.wait_ge(count_ready, l + 1)
                T.matmul(pre_ps, before[0:EP, 0:EP], count[:, :], start=True, stop=True)
                T.matmul(tot_ps, ones[0:EP, :], count[:, :], start=True, stop=True).then_inc(prefix_done, 1)
                pe.wait_ge(tileof_ready, l + 1)
                for q in range(4):
                    w = min(P, CHP - q * P)
                    last = T.matmul(ps[0:1, 7, q * P:q * P + w], tile_of[:, q:q + 1], ident[:, 0:w], start=True, stop=True)
                last.then_inc(tilerow_done, 1)
                pe.wait_ge(toff_ready, l + 1)

            def sort_column(l, n, s):
                pe.wait_ge(hot_ready, n)
                for k, c0, c1, where in sort_regions[l]:
                    last = T.matmul(where, place_val[:, s, k, :], chunk_hot[:, s, c0:c1], start=False, stop=False,
                                    skip_group_check=True)
                return last

            def add_up(l, sorting):
                with nc.tensor.Fori(0, ROUNDS) as r:
                    col = 0
                    for g in range(GROUPS):
                        _, offs = nc.values_load_multi_w_load_instructions(
                            tile_off[l][0:1, bass.ds(r * GROUPS + g, 1), 0:GROUP].rearrange("p g i -> p (g i)"),
                            engines=[mybir.EngineType.PE], min_val=0, max_val=(TILES - 1) * D,
                            skip_runtime_bounds_check_because="tile_of is cut to the last tile")
                        pe.wait_ge(got[l][g], r * (16 * GROUP) + 16 * GROUP)
                        for i in range(GROUP):
                            k = g * GROUP + i
                            pe.wait_ge(nhot_ready, r * RING + (l * CHP + k + 1))
                            T.matmul(psf[0:NP, bass.ds(offs[i], D)], node_hot[:, k % HOTS, :], gathered[:, k, :],
                                     start=False, stop=False, skip_group_check=True).then_inc(nhot_used, 1)
                        if sorting:
                            for _ in range(SORT_IN_GROUP[g]):
                                sort_column(1, r * SORT_PER_ROUND + (EC + col + 1), col % SORT_BUFS).then_inc(hot_used, 1)
                                col += 1

            rank_sums(0)
            zero_bank(7)
            zero_bank(0)
            with nc.tensor.Fori(0, EC // SORT_BUFS) as r:
                for c in range(SORT_BUFS):
                    sort_column(0, r * SORT_BUFS + (c + 1), c).then_inc(hot_used, 1)
            pe.wait_ge(decoded, 1)
            for b in range(NBANK):
                zero_bank(b)
            rank_sums(1)
            zero_bank(7)
            add_up(0, True)
            pe.wait_ge(decoded, 2)
            pe.wait_ge(ld_w, 96)
            T.transpose(ps[:, 7, 0:D], ws_sb[:, :], ident[:, :]).then_inc(wsT_ps, 1)
            pe.wait_ge(wsT_ready, 1)
            pe.wait_ge(rst_ready, NBANK)

            def turn(g):
                a0, a1 = groups[g]
                for t in range(a0, a1):
                    last = T.transpose(ps[:, g % 2, (t - a0) * NP:(t - a0 + 1) * NP], h_sb[:, t, :], ident[0:NP, 0:NP])
                last.then_inc(featT_ps, 1)

            def first(g):
                w = (groups[g][1] - groups[g][0]) * NP
                pe.wait_ge(featT_ready, g + 1)
                T.matmul(ps[:, 2 + g % 2, 0:w], w1_sb[:, :], featT[:, g % 2, 0:w], start=True, stop=True).then_inc(hid_ps, 1)

            def second(g):
                a0, a1 = groups[g]
                pe.wait_ge(hid_ready, g + 1)
                if g >= 2:
                    pe.wait_ge(y_used, g - 1)
                for t in range(a0, a1):
                    c = (t - a0) * D
                    T.matmul(ps[0:NP, 4 + g % 2, c:c + D], hidT[:, g % 2, (t - a0) * NP:(t - a0 + 1) * NP], w2_sb[:, :],
                             start=True, stop=False)
                    last = T.matmul(ps[0:NP, 4 + g % 2, c:c + D], ones[0:1, 0:NP], b2_sb[:, :], start=False, stop=True)
                last.then_inc(y_ps, 1)

            for g in range(NBANK + 2):
                if g < NBANK:
                    turn(g)
                if 1 <= g <= NBANK:
                    first(g - 1)
                if g >= 2:
                    second(g - 2)

            pe.wait_ge(h_ready, 2)
            for g, (a0, a1) in enumerate(groups):
                if g >= 2:
                    pe.wait_ge(h2T_ready, g - 1)
                for t in range(a0, a1):
                    last = T.transpose(ps[:, g % 2, (t - a0) * NP:(t - a0 + 1) * NP], h_sb[:, t, :], ident[0:NP, 0:NP])
                last.then_inc(h2T_ps, 1)
            pe.wait_ge(h2T_ready, NBANK)
            pe.wait_ge(wrel_ready, N_REL * N_BASES)
            for n in range(2 * TILES):
                t, half = divmod(n, 2)
                m = n - 4
                if m >= 0:
                    if m % 2 == 0:
                        pe.wait_ge(z_even, m // 2 + 1)
                    else:
                        pe.wait_ge(z_odd, m // 2 + 1)
                for q in range(2):
                    last = T.matmul(ps[0:NP, (n % 4) * 2 + q, :], h2T[:, t * NP:(t + 1) * NP],
                                    w_rel[:, half * 8 + q * 4:half * 8 + q * 4 + 4, :], start=True, stop=True)
                last.then_inc(z_ps, 1)
            pe.wait_ge(z_even, TILES)
            pe.wait_ge(z_odd, TILES)
            for g, (a0, a1) in enumerate(groups):
                for t in range(a0, a1):
                    last = T.matmul(ps[0:NP, g, (t - a0) * D:(t - a0 + 1) * D], h2T[:, t * NP:(t + 1) * NP], wsT[:, :],
                                    start=True, stop=True)
                last.then_inc(self_ps, 1)
            pe.wait_ge(self_used, NBANK)
            for b in range(NBANK):
                zero_bank(b)
            add_up(1, False)


_INS = ["x", "src", "dst", "edge_type_16", "L0_gnn_eps", "L0_gnn_W1", "L0_gnn_b1", "L0_gnn_W2", "L0_gnn_b2",
        "L1_gnn_bases", "L1_gnn_coefficients", "L1_gnn_w_self"]


def kernel(**inputs):
    import concourse.bacc as _bacc
    from concourse.bass_utils import run_bass_kernel_spmd as _run

    nc = _bacc.Bacc("TRN2", target_bir_lowering=False, num_devices=1)
    arrays, args = {}, []
    for name in _INS:
        a = np.ascontiguousarray(inputs[name])
        arrays[f"in_{name}"] = a
        args.append(nc.dram_tensor(f"in_{name}", a.shape, mybir.dt.from_np(a.dtype), kind="ExternalInput").ap())
    out = nc.dram_tensor("out", (N_NODES, D), F32, kind="ExternalOutput").ap()
    build(nc, *args, out)
    r = _run(nc, [arrays], core_ids=[0])
    return r.results[0]["out"]
```

```python
import numpy as np
import concourse.bass as bass
from concourse import mybir
from contextlib import ExitStack

F32 = mybir.dt.float32
F16 = mybir.dt.float16
BF16 = mybir.dt.bfloat16
I32 = mybir.dt.int32
ALU = mybir.AluOpType
ACT = mybir.ActivationFunctionType
AX = mybir.AxisListType

N_NODES, N_EDGES, D, N_REL, N_BASES = 3125, 50000, 128, 16, 8
P = 128

TILES = 25
NP = N_NODES // TILES
DIV_MUL, DIV_SHIFT = 5243, 17

EC = 400
EP = N_EDGES // EC

GROUPS = 4
SORTS = [(0, 0, 155, 11), (0, 155, 245, 11), (1, 0, 400, 13)]
COLS = [cols for _, _, cols, _ in SORTS]
GROUP = [group for _, _, _, group in SORTS]
RING = [GROUPS * group for group in GROUP]
MOST = [(EP * cols + TILES * (P - 1)) // P for cols in COLS]
ROUNDS = [-(-most // ring) for most, ring in zip(MOST, RING)]
CHUNKS = [rounds * ring for rounds, ring in zip(ROUNDS, RING)]
CHUNKS_BEFORE = [sum(CHUNKS[:s]) for s in range(3)]
COLS_BEFORE = [sum(COLS[:s]) for s in range(3)]
WIDEST = max(CHUNKS)
HOTS = [2 * group for group in GROUP]
GROW = 16
BATCH = 5
RUN = BATCH + 1
BATCH_BUFS = 2
BESIDE_ROUNDS = [0, 4, 5]
BATCHES_IN_GROUP = [0] + [COLS[s] // (BATCH * GROUPS * BESIDE_ROUNDS[s]) for s in (1, 2)]
PER_ROUND = [n * GROUPS for n in BATCHES_IN_GROUP]
AHEAD = [COLS[s] // BATCH - BESIDE_ROUNDS[s] * PER_ROUND[s] for s in range(3)]
BATCHES_BEFORE = [c // BATCH for c in COLS_BEFORE]
assert all(n % BATCH_BUFS == 0 for n in PER_ROUND) and all(c % BATCH == 0 for c in COLS)

BIG = 1000.0

BANK = 512
BT = BANK // D
NBANK = -(-TILES // BT)
SPLIT = 112
EPS = 1e-5
Z_LAG = 6


def build(nc, x, src, dst, etype, eps, W1, b1, W2, b2, bases, coef, w_self, out):
    ctx = ExitStack()
    with ctx:
        def sb(name, shape, dt):
            return ctx.enter_context(nc.sbuf_tensor(name, shape, dt))

        def sem(name):
            return ctx.enter_context(nc.semaphore(name))

        h_table = nc.dram_tensor("h_table", [N_NODES, D], F32).ap()
        z_table = nc.dram_tensor("z_table", [N_NODES * N_REL, D], F32).ap()

        iota_i = sb("iota_i", [P, BANK], I32)
        pidx_i = sb("pidx_i", [P, 4], I32)
        iota_f = sb("iota_f", [P, BANK], F32)
        iota_h = sb("iota_h", [P, BANK], F16)
        iota_run = sb("iota_run", [P, P, RUN], F16)
        pidx = sb("pidx", [P, 4], F32)
        ident = sb("ident", [P, P], F32)
        before = sb("before", [P, P], F32)
        ones = sb("ones", [P, P], F32)
        zeros_h = sb("zeros_h", [P, P], F16)
        w1_sb = sb("w1_sb", [D, D], F32)
        w2_sb = sb("w2_sb", [D, D], F32)
        ws_sb = sb("ws_sb", [D, D], F32)
        wsT = sb("wsT", [D, D], F32)
        b1_sb = sb("b1_sb", [D, 1], F32)
        b2_sb = sb("b2_sb", [NP, 1, D], F32)
        eps1 = sb("eps1", [P, 1], F32)
        coef_sb = sb("coef_sb", [P, N_REL * N_BASES], F32)
        bases_sb = sb("bases_sb", [D, N_BASES, D], F32)
        w_rel = sb("w_rel", [D, N_REL, D], F32)
        ends_i = [sb("dst_i", [EP, EC], I32), sb("src_i", [EP, EC], I32)]
        dst_i, src_i = ends_i
        type_i = sb("type_i", [EP, EC], I32)
        t0 = sb("t0", [EP, EC], I32)
        t1 = sb("t1", [EP, EC], I32)
        low_i = sb("low_i", [EP, EC], I32)
        tile_h = sb("tile_h", [EP, EC], F16)
        row_i = sb("row_i", [EP, EC], I32)
        member_flat = sb("member", [EP, TILES * EC], BF16)
        spare = sb("spare", [P, TILES * EC], F32)
        pos_i = sb("pos_i", [EP, EC], I32)
        chunk_f = [sb(f"chunk_f{l}", [EP, EC], F32) for l in range(2)]
        place_h = [sb(f"place_h{l}", [EP, EC + RUN - BATCH], F16) for l in range(2)]
        code_a = [sb(f"code_a{l}", [EP, EC + RUN - BATCH], F16) for l in range(2)]
        code_b = [sb(f"code_b{l}", [EP, EC], F32) for l in range(2)]
        count = sb("count", [EP, TILES], F32)
        lower = sb("lower", [EP, TILES], F32)
        adjust = sb("adjust", [EP, TILES], F32)
        need_i = sb("need_i", [P, TILES], I32)
        need_f = sb("need_f", [P, TILES], F32)
        upto = sb("upto", [P, TILES], F32)
        le_scr = sb("le_scr", [P, TILES], F32)
        tile_of = sb("tile_of", [P, 4], F32)
        tile_off = [sb(f"tile_off{s}", [1, ROUNDS[s] * GROUPS, GROW], I32) for s in range(3)]
        chunk_hot = sb("chunk_hot", [EP, BATCH_BUFS, BATCH, WIDEST], F16)
        place_hot = sb("place_hot", [EP, BATCH_BUFS, P, RUN], F16)
        place_val_a = sb("place_val_a", [EP, BATCH_BUFS, P, RUN], F16)
        place_val_b = sb("place_val_b", [EP, BATCH_BUFS, BATCH, P], F16)
        s0 = sb("s0", [P, WIDEST], I32)
        s1 = sb("s1", [P, WIDEST], I32)
        s2 = sb("s2", [P, WIDEST], I32)
        pad_f = sb("pad_f", [P, WIDEST], F32)
        row_of = [sb(f"row_of{s}", [P, CHUNKS[s]], I32) for s in range(3)]
        key_of = [sb(f"key_of{s}", [P, CHUNKS[s]], F32) for s in range(3)]
        row_stage = sb("row_stage", [P, GROUPS, max(GROUP)], I32)
        gathered = sb("gathered", [P, max(RING), D], F32)
        node_hot = sb("node_hot", [P, max(HOTS), NP], F32)
        x_sb = sb("x_sb", [NP, TILES, D], F32)
        h_sb = sb("h_sb", [NP, TILES, D], F32)
        stats = sb("stats", [NP, TILES, 6], F32)
        mv = sb("mv", [NP, TILES, 2], F32)
        sd = sb("sd", [NP, TILES], F32)
        rstd = sb("rstd", [NP, TILES], F32)
        epsc = sb("epsc", [P, 1], F32)
        w_part = spare[:, 7400:7400 + N_REL * D].rearrange("p (r d) -> p r d", d=D)
        z_stage = spare[0:NP, 0:4 * 1024].rearrange("p (s n) -> p s n", s=4)
        h2T = spare[:, 4096:4096 + TILES * NP]
        featT = spare[:, 7400:7900]
        hidT = spare[:, 7900:8400]
        y_sum = spare[0:NP, 8400:8400 + BT * D].rearrange("p (t d) -> p t d", d=D)

        ps = ctx.enter_context(nc.psum_tensor("ps", [P, 8, BANK], F32))
        psf = ps[:, :, :].rearrange("p b c -> p (b c)")
        LASTB = NBANK - 1
        USED = (TILES - BT * LASTB) * D
        pre_ps = ps[0:EP, 7, 448:448 + TILES]
        tot_ps = ps[:, 7, 480:480 + TILES]
        room = BANK - USED
        sort_regions = []
        for w in CHUNKS:
            parts = [(0, 0, w, ps[:, 7, 0:w]), (1, 0, min(w, room), ps[:, LASTB, USED:USED + min(w, room)])]
            if w > room:
                parts.append((1, room, w, ps[:, 7, w:w + w - room]))
            sort_regions.append(parts)

        ld_edge, ld_x, ld_w, ld_c = sem("ld_edge"), sem("ld_x"), sem("ld_w"), sem("ld_c")
        iota_done = sem("iota_done")
        consts_done = sem("consts_done")
        v = sem("v")
        a = sem("a")
        count_ready = sem("count_ready")
        prefix_done = sem("prefix_done")
        tileof_ready = sem("tileof_ready")
        tilerow_done = sem("tilerow_done")
        toff_ready = sem("toff_ready")
        place_ready = sem("place_ready")
        chunk_ready = sem("chunk_ready")
        val_ready = sem("val_ready")
        batch_used = sem("batch_used")
        sorted_read = sem("sorted_read")
        decoded = sem("decoded")
        staged = [[sem(f"staged{l}_{g}") for g in range(GROUPS)] for l in range(3)]
        begun = sem("begun")
        got = [[sem(f"got{l}_{g}") for g in range(GROUPS)] for l in range(3)]
        nhot_ready = sem("nhot_ready")
        nhot_used = sem("nhot_used")
        var_ready = sem("var_ready")
        sd_ready = sem("sd_ready")
        norm_ready = sem("norm_ready")
        h_ready = sem("h_ready")
        h_stored = sem("h_stored")
        rst_ready = sem("rst_ready")
        featT_ps = sem("featT_ps")
        featT_ready = sem("featT_ready")
        hid_ps = sem("hid_ps")
        hid_ready = sem("hid_ready")
        y_ps = sem("y_ps")
        y_used = sem("y_used")
        h2T_ps = sem("h2T_ps")
        h2T_ready = sem("h2T_ready")
        wsT_ps = sem("wsT_ps")
        wsT_ready = sem("wsT_ready")
        wrel_ready = sem("wrel_ready")
        z_ps = sem("z_ps")
        z_even, z_odd = sem("z_even"), sem("z_odd")
        z_stored = [sem(f"z_stored{s}") for s in range(4)]
        self_ps = sem("self_ps")
        self_used = sem("self_used")
        out_ready = sem("out_ready")
        out_stored = sem("out_stored")

        x_rows = x.rearrange("(p t) d -> p t d", t=TILES)
        h_rows = h_table.rearrange("(p t) d -> p t d", t=TILES)
        z_rows = z_table.rearrange("(p t r) d -> p t (r d)", t=TILES, r=N_REL)
        out_rows = out.rearrange("(p t) d -> p t d", t=TILES)
        PARTS = ((0, SPLIT), (SPLIT, NP))
        groups = [(BT * g, min(TILES, BT * (g + 1))) for g in range(NBANK)]

        def z_half(n):
            return psf[0:NP, (4 + 2 * (n % 2)) * BANK:(6 + 2 * (n % 2)) * BANK]

        def batches_ahead(engine, s, sort_batch):
            buf = BATCHES_BEFORE[s]
            turns = AHEAD[s] // BATCH_BUFS
            if turns:
                with engine.Fori(0, turns) as r:
                    for b in range(BATCH_BUFS):
                        sort_batch(s, r * BATCH_BUFS + b, (buf + b) % BATCH_BUFS)
            for b in range(turns * BATCH_BUFS, AHEAD[s]):
                sort_batch(s, b, (buf + b) % BATCH_BUFS)

        def rounds(engine, s, group_work, sort_batch):
            beside = BESIDE_ROUNDS[s + 1] if s < 2 else 0
            if beside:
                with engine.Fori(0, beside) as r:
                    for g in range(GROUPS):
                        group_work(s, g, r)
                        for b in range(g * BATCHES_IN_GROUP[s + 1], (g + 1) * BATCHES_IN_GROUP[s + 1]):
                            sort_batch(s + 1, r * PER_ROUND[s + 1] + (AHEAD[s + 1] + b),
                                       (BATCHES_BEFORE[s + 1] + AHEAD[s + 1] + b) % BATCH_BUFS)
            if beside < ROUNDS[s]:
                with engine.Fori(beside, ROUNDS[s]) as r:
                    for g in range(GROUPS):
                        group_work(s, g, r)

        block = ctx.enter_context(nc.Block())

        def stage_rows(sp, s):
            sp.wait_ge(decoded, s + 1)
            with nc.sync.Fori(0, ROUNDS[s]) as r:
                for g in range(GROUPS):
                    sp.wait_ge(nhot_used, r * RING[s] + (CHUNKS_BEFORE[s] + (g + 1) * GROUP[s] + RING[0] - RING[s]))
                    sp.dma_start(row_stage[:, g, 0:GROUP[s]],
                                 row_of[s][:, bass.ds(r * RING[s] + g * GROUP[s], GROUP[s])]).then_inc(staged[s][g], 16)

        @block.sync
        def _(sp):
            for t, d in ((dst_i, dst), (src_i, src), (type_i, etype)):
                sp.dma_start(t[:, :], d.rearrange("(p c) -> p c", c=EC)).then_inc(ld_edge, 16)
            for p0, p1 in PARTS:
                sp.dma_start(x_sb[p0:p1, :, :], x_rows[p0:p1, :, :]).then_inc(ld_x, 16)
            sp.dma_start(w1_sb[:, :], W1).then_inc(ld_w, 16)
            sp.dma_start(w2_sb[:, :], W2).then_inc(ld_w, 16)
            sp.dma_start(ws_sb[:, :], w_self).then_inc(ld_w, 16)
            sp.dma_start(b1_sb[:, :], b1.rearrange("(p o) -> p o", o=1)).then_inc(ld_w, 16)
            sp.dma_start(b2_sb[:, 0, :], b2.rearrange("(o d) -> o d", o=1).to_broadcast([NP, D])).then_inc(ld_w, 16)
            sp.dma_start(eps1[:, :], eps.rearrange("(o d) -> o d", o=1).to_broadcast([P, 1])).then_inc(ld_w, 16)
            sp.dma_start(coef_sb[:, :], coef.rearrange("(o r) b -> o (r b)", o=1).to_broadcast([P, N_REL * N_BASES])).then_inc(ld_c, 16)
            sp.dma_start(bases_sb[:, :, :], bases.rearrange("b i o -> i b o")).then_inc(ld_c, 16)
            sp.wait_ge(h_ready, 1)
            for p0, p1 in PARTS:
                sp.dma_start(h_rows[p0:p1, :, :], h_sb[p0:p1, :, :]).then_inc(h_stored, 16)
            stage_rows(sp, 0)
            stage_rows(sp, 1)
            for t in range(TILES):
                for half in range(2):
                    slot = (2 * t + half) % 4
                    if half == 0:
                        sp.wait_ge(z_even, t + 1)
                    else:
                        sp.wait_ge(z_odd, t + 1)
                    for p0, p1 in PARTS:
                        sp.dma_start(z_rows[p0:p1, t, half * 1024:(half + 1) * 1024],
                                     z_stage[p0:p1, slot, :]).then_inc(z_stored[slot], 16)
            stage_rows(sp, 2)
            for g in range(NBANK):
                sp.wait_ge(out_ready, g + 1)
                a0, a1 = groups[g]
                for p0, p1 in PARTS:
                    sp.dma_start(out_rows[p0:p1, a0:a1, :], x_sb[p0:p1, a0:a1, :]).then_inc(out_stored, 16)
            sp.wait_ge(out_stored, 32 * NBANK)

        @block.gpsimd
        def _(pool):
            pool.iota(iota_i[:, :], [[1, BANK]], base=0, channel_multiplier=0).then_inc(iota_done, 1)
            pool.iota(pidx_i[:, :], [[P, 4]], base=0, channel_multiplier=1).then_inc(iota_done, 1)
            pool.wait_ge(ld_c, 32)
            for b in range(N_BASES):
                base = bases_sb[:, b:b + 1, :].to_broadcast([D, N_REL, D])
                share = coef_sb[:, :].rearrange("p (r b) -> p r b", b=N_BASES)[:, :, b:b + 1].to_broadcast([D, N_REL, D])
                pool.tensor_tensor((w_part if b else w_rel)[:, :, :], base, share, ALU.mult).then_inc(wrel_ready, 1)
                if b:
                    pool.wait_ge(wrel_ready, 2 * b)
                    pool.tensor_tensor(w_rel[:, :, :], w_rel[:, :, :], w_part[:, :, :], ALU.add).then_inc(wrel_ready, 1)
                    pool.wait_ge(wrel_ready, 2 * b + 1)
            for s in range(3):
                table = h_table if s < 2 else z_table
                if s == 2:
                    for q in range(3):
                        pool.wait_ge(z_stored[q], 32 * ((2 * TILES - q + 3) // 4))
                with nc.gpsimd.Fori(0, ROUNDS[s]) as r:
                    for g in range(GROUPS):
                        if s < 2:
                            pool.wait_ge(h_stored, 32)
                        else:
                            pool.wait_ge(z_stored[3], 32 * ((2 * TILES - 3 + 3) // 4))
                        pool.wait_ge(staged[s][g], r * 16 + 16)
                        pool.sem_inc(begun, 1)
                        for i in range(GROUP[s]):
                            pool.indirect_dma_start(
                                gathered[:, g * GROUP[s] + i, :], None, table,
                                bass.IndirectOffsetOnAxis(ap=row_stage[:, g, i:i + 1], axis=0)).then_inc(got[s][g], 16)

        @block.scalar
        def _(act):
            done = 0

            def own(ins):
                nonlocal done
                ins.then_inc(a, 1)
                done += 1
                act.wait_ge(a, done)

            act.wait_ge(consts_done, 1)
            act.wait_ge(var_ready, 1)
            nc.scalar.activation(sd[:, :], mv[:, :, 1], ACT.Sqrt, bias=epsc[0:NP, :]).then_inc(sd_ready, 1)
            act.wait_ge(norm_ready, 1)
            nc.scalar.activation(h_sb[:, :, :], h_sb[:, :, :], ACT.Relu).then_inc(h_ready, 1)

            def sort_batch(s, batch, buf):
                l, c0, _, _ = SORTS[s]
                act.wait_ge(place_ready, batch + (BATCHES_BEFORE[s] + 1))
                for i in range(BATCH):
                    nc.scalar.activation(place_val_b[:, buf, i, :], place_hot[:, buf, :, i], ACT.Copy,
                                         scale=code_b[l][:, bass.ds(batch * BATCH + (c0 + i), 1)]).then_inc(val_ready, 1)

            batches_ahead(nc.scalar, 0, sort_batch)
            for s in (1, 2):
                batches_ahead(nc.scalar, s, sort_batch)
                with nc.scalar.Fori(0, BESIDE_ROUNDS[s]) as r:
                    for b in range(PER_ROUND[s]):
                        sort_batch(s, r * PER_ROUND[s] + (AHEAD[s] + b), (BATCHES_BEFORE[s] + AHEAD[s] + b) % BATCH_BUFS)
            for step in range(NBANK + Z_LAG):
                g = step - 1
                if 0 <= g < NBANK:
                    act.wait_ge(hid_ps, g + 1)
                    w = (groups[g][1] - groups[g][0]) * NP
                    nc.scalar.activation(hidT[:, 0:w], ps[:, 2, 0:w], ACT.Relu, bias=b1_sb[:, :]).then_inc(hid_ready, 1)
                g = step
                if 0 <= g < NBANK:
                    act.wait_ge(featT_ps, g + 1)
                    w = (groups[g][1] - groups[g][0]) * NP
                    nc.scalar.copy(featT[:, 0:w], ps[:, g % 2, 0:w]).then_inc(featT_ready, 1)
                g = step - 3
                if 0 <= g < NBANK:
                    a0, a1 = groups[g]
                    act.wait_ge(var_ready, g + 2)
                    nc.scalar.activation(sd[:, a0:a1], mv[:, a0:a1, 1], ACT.Sqrt, bias=epsc[0:NP, :]).then_inc(sd_ready, 1)
                g = step - 4
                if 0 <= g < NBANK:
                    a0, a1 = groups[g]
                    act.wait_ge(norm_ready, g + 2)
                    nc.scalar.activation(h_sb[:, a0:a1, :], h_sb[:, a0:a1, :], ACT.Relu).then_inc(h_ready, 1)
                g = step - 5
                if 0 <= g < NBANK:
                    a0, a1 = groups[g]
                    act.wait_ge(h2T_ps, g + 1)
                    nc.scalar.copy(h2T[:, a0 * NP:a1 * NP], ps[:, g % 2, 0:(a1 - a0) * NP]).then_inc(h2T_ready, 1)
                g = step - Z_LAG
                if 0 <= g < NBANK:
                    for t in range(*groups[g]):
                        n = 2 * t + 1
                        act.wait_ge(z_ps, n + 1)
                        if n >= 4:
                            act.wait_ge(z_stored[n % 4], 32 * (n // 4))
                        nc.scalar.copy(z_stage[:, n % 4, :], z_half(n)).then_inc(z_odd, 1)

        @block.vector
        def _(dve):
            done = 0

            def own(ins):
                nonlocal done
                ins.then_inc(v, 1)
                done += 1
                dve.wait_ge(v, done)

            V = nc.vector
            dve.wait_ge(iota_done, 2)
            V.tensor_copy(iota_f[:, :], iota_i[:, :])
            V.tensor_copy(iota_h[:, :], iota_i[:, :])
            V.memset(ones[:, :], 1.0)
            V.memset(zeros_h[:, :], 0.0)
            V.memset(epsc[:, :], EPS)
            for l in range(2):
                V.memset(place_h[l][:, :], 0.0)
                V.memset(code_a[l][:, :], 0.0)
            V.tensor_copy(iota_run[:, :, :],
                          iota_i[:, 0:P].rearrange("p (v o) -> p v o", o=1).to_broadcast([P, P, RUN]))
            own(V.tensor_copy(pidx[:, :], pidx_i[:, :]))
            V.tensor_scalar(ident[:, :], iota_f[:, 0:P], pidx[:, 0:1], None, ALU.is_equal)
            V.tensor_scalar(before[:, :], iota_f[:, 0:P], pidx[:, 0:1], None, ALU.is_gt).then_inc(consts_done, 1)

            def norm(n, a0, a1):
                dve.wait_ge(sd_ready, n + 1)
                own(V.reciprocal(rstd[:, a0:a1], sd[:, a0:a1]))
                for t in range(a0, a1):
                    last = V.tensor_scalar(h_sb[:, t, :], x_sb[:, t, :], mv[:, t, 0:1], rstd[:, t:t + 1],
                                           ALU.subtract, ALU.mult)
                last.then_inc(norm_ready, 1)

            def mean_var(a0, a1):
                for t in range(a0, a1):
                    last = V.bn_stats(stats[:, t, :], x_sb[:, t, :])
                own(last)
                for t in range(a0, a1):
                    last = V.bn_aggr(mv[:, t, :], stats[:, t, :])
                last.then_inc(var_ready, 1)

            dve.wait_ge(ld_x, 32)
            mean_var(0, TILES)
            norm(0, 0, TILES)

            dve.wait_ge(ld_edge, 48)

            def rank(s):
                l, c0, cols, _ = SORTS[s]
                cs = slice(c0, c0 + cols)
                key = ends_i[l][:, cs]
                row = (src_i if l == 0 else row_i)[:, cs]
                low, scr0, scr1, spot = low_i[:, cs], t0[:, cs], t1[:, cs], pos_i[:, cs]
                member_f = member_flat[:, 0:TILES * cols]
                running_f = spare[0:EP, 0:TILES * cols]
                member = member_f.rearrange("p (b c) -> p b c", c=cols)
                running = running_f.rearrange("p (b c) -> p b c", c=cols)
                if l == 1:
                    dve.wait_ge(wrel_ready, 2 * N_BASES - 1)
                    own(V.scalar_tensor_tensor(row, dst_i[:, cs], float(N_REL), type_i[:, cs], ALU.mult, ALU.add))
                own(V.tensor_scalar(scr0, key, float(DIV_MUL), None, ALU.mult))
                own(V.tensor_scalar(low, scr0, DIV_SHIFT, None, ALU.logical_shift_right))
                own(V.scalar_tensor_tensor(tile_h[:, cs], low, -float(TILES), key, ALU.mult, ALU.add))
                for b in range(TILES):
                    last = V.tensor_scalar(member[:, b, :], tile_h[:, cs], float(b), None, ALU.is_equal)
                own(last)
                own(V.tensor_tensor_scan(running_f, member_f, member_f, 0.0, ALU.add, ALU.bypass))
                V.tensor_copy(count[:, 0:1], running[:, 0, cols - 1:cols])
                V.tensor_tensor(count[:, 1:TILES], running[:, 1:TILES, cols - 1], running[:, 0:TILES - 1, cols - 1],
                                ALU.subtract).then_inc(count_ready, 1)
                dve.wait_ge(prefix_done, s + 1)
                dve.wait_ge(count_ready, s + 1)
                V.tensor_copy(lower[:, :], pre_ps)
                own(V.tensor_scalar(need_i[:, :], tot_ps, float(P - 1), None, ALU.add))
                own(V.tensor_scalar(need_i[:, :], need_i[:, :], 7, None, ALU.logical_shift_right))
                own(V.tensor_copy(need_f[:, :], need_i[:, :]))
                own(V.tensor_tensor_scan(upto[:, :], need_f[:, :], need_f[:, :], 0.0, ALU.add, ALU.bypass))
                for q in range(4):
                    own(V.tensor_scalar(le_scr[:, :], upto[:, :], pidx[:, q:q + 1], 0.0, ALU.is_le, ALU.add,
                                        accum_out=tile_of[:, q:q + 1]))
                V.tensor_scalar(tile_of[:, :], tile_of[:, :], float(TILES - 1), float(D), ALU.min, ALU.mult).then_inc(tileof_ready, 1)
                own(V.tensor_tensor(need_f[:, :], upto[:, :], need_f[:, :], ALU.subtract))
                own(V.scalar_tensor_tensor(adjust[:, :], need_f[0:EP, :], float(P), lower[:, :], ALU.mult, ALU.add))
                own(V.scalar_tensor_tensor(adjust[:, :], adjust[:, :], -1.0, count[:, :], ALU.add, ALU.add))
                own(V.tensor_tensor(adjust[:, :], adjust[:, :], running[:, :, cols - 1], ALU.subtract))
                for b in range(TILES):
                    last = V.scalar_tensor_tensor(running[:, b, :], running[:, b, :], adjust[:, b:b + 1], member[:, b, :],
                                                  ALU.add, ALU.mult)
                own(last)
                own(V.tensor_reduce(chunk_f[l][:, cs], running.rearrange("p b c -> p c b"), AX.X, ALU.add))
                own(V.tensor_copy(spot, chunk_f[l][:, cs]))
                V.tensor_scalar(scr0, spot, 7, None, ALU.logical_shift_right)
                own(V.tensor_scalar(scr1, spot, P - 1, None, ALU.bitwise_and))
                V.tensor_copy(chunk_f[l][:, cs], scr0)
                own(V.tensor_copy(place_h[l][:, cs], scr1))
                V.tensor_scalar(scr0, row, 8, 3, ALU.logical_shift_right, ALU.logical_shift_left)
                own(V.tensor_scalar(scr1, low, 4, None, ALU.logical_shift_right))
                own(V.scalar_tensor_tensor(code_a[l][:, cs], scr0, 1.0, scr1, ALU.add, ALU.add))
                V.tensor_scalar(scr0, row, 255, 4, ALU.bitwise_and, ALU.logical_shift_left)
                own(V.tensor_scalar(scr1, low, 15, None, ALU.bitwise_and))
                own(V.scalar_tensor_tensor(code_b[l][:, cs], scr0, -2048.0, scr1, ALU.add, ALU.add))
                dve.wait_ge(tilerow_done, s + 1)
                V.tensor_copy(tile_off[s][:, :, 0:GROUP[s]],
                              ps[0:1, 7, 0:CHUNKS[s]].rearrange("p (g i) -> p g i", i=GROUP[s])).then_inc(toff_ready, 1)

            def sort_batch(s, batch, buf):
                l, c0, _, _ = SORTS[s]
                dve.wait_ge(batch_used, batch + (BATCHES_BEFORE[s] + 1))
                run = bass.ds(batch * BATCH + c0, RUN)
                V.tensor_tensor(place_hot[:, buf, :, :], iota_run[0:EP, :, :],
                                place_h[l][:, run].rearrange("p (o c) -> p o c", o=1).to_broadcast([EP, P, RUN]),
                                ALU.is_equal).then_inc(place_ready, 1)
                dve.wait_ge(place_ready, batch + (BATCHES_BEFORE[s] + 1))
                V.tensor_tensor(place_val_a[:, buf, :, :], place_hot[:, buf, :, :],
                                code_a[l][:, run].rearrange("p (o c) -> p o c", o=1).to_broadcast([EP, P, RUN]),
                                ALU.mult)
                for i in range(BATCH):
                    V.tensor_scalar(chunk_hot[:, buf, i, 0:CHUNKS[s]], iota_h[0:EP, 0:CHUNKS[s]],
                                    chunk_f[l][:, bass.ds(batch * BATCH + (c0 + i), 1)],
                                    None, ALU.is_equal).then_inc(chunk_ready, 1)

            def read_sorted(s):
                dve.wait_ge(batch_used, BATCH_BUFS + BATCHES_BEFORE[s] + COLS[s] // BATCH)
                dve.wait_ge(nhot_used, RING[0] + CHUNKS_BEFORE[s])
                w = CHUNKS[s]
                pa = ps[:, 7, 0:w]
                V.tensor_scalar(s0[:, 0:w], pa, -1.0, 0.0, ALU.add, ALU.max)
                last = V.tensor_scalar(pad_f[:, 0:w], pa, 0.0, BIG, ALU.is_equal, ALU.mult)
                for k, c0, c1, where in sort_regions[s]:
                    if k == 1:
                        last = V.tensor_scalar(s1[:, c0:c1], where, 2048.0, None, ALU.add)
                last.then_inc(sorted_read, 1)
                dve.wait_ge(sorted_read, s + 1)
                if s < 2:
                    V.memset(ps[:, LASTB, USED:BANK], 0.0)

            def decode(s):
                w = CHUNKS[s]
                own(V.tensor_scalar(s2[:, 0:w], s0[:, 0:w], 3, 8, ALU.logical_shift_right, ALU.logical_shift_left))
                own(V.tensor_scalar(row_of[s][:, :], s1[:, 0:w], 4, None, ALU.logical_shift_right))
                V.tensor_tensor(row_of[s][:, :], row_of[s][:, :], s2[:, 0:w], ALU.add).then_inc(decoded, 1)
                dve.wait_ge(decoded, s + 1)
                own(V.tensor_scalar(s0[:, 0:w], s0[:, 0:w], 7, 4, ALU.bitwise_and, ALU.logical_shift_left))
                own(V.tensor_scalar(s1[:, 0:w], s1[:, 0:w], 15, None, ALU.bitwise_and))
                own(V.tensor_tensor(pad_f[:, 0:w], pad_f[:, 0:w], s0[:, 0:w], ALU.add))
                own(V.tensor_tensor(key_of[s][:, :], pad_f[:, 0:w], s1[:, 0:w], ALU.add))

            def node_hots(s, g, r):
                dve.wait_ge(nhot_used, r * RING[s] + (CHUNKS_BEFORE[s] + (g + 1) * GROUP[s] + RING[0] - HOTS[s]))
                for i in range(GROUP[s]):
                    k = g * GROUP[s] + i
                    V.tensor_scalar(node_hot[:, k % HOTS[s], :], iota_f[:, 0:NP], key_of[s][:, bass.ds(r * RING[s] + k, 1)],
                                    None, ALU.is_equal).then_inc(nhot_ready, 1)

            rank(0)
            batches_ahead(nc.vector, 0, sort_batch)
            for s in (1, 2):
                read_sorted(s - 1)
                decode(s - 1)
                rank(s)
                batches_ahead(nc.vector, s, sort_batch)
                rounds(nc.vector, s - 1, node_hots, sort_batch)

            dve.wait_ge(ld_w, 96)
            own(V.tensor_scalar(eps1[:, :], eps1[:, :], 1.0, None, ALU.add))
            dve.wait_ge(nhot_used, RING[0] + CHUNKS_BEFORE[2])
            for g, (a0, a1) in enumerate(groups):
                V.scalar_tensor_tensor(h_sb[:, a0:a1, :], h_sb[:, a0:a1, :], eps1[0:NP, :],
                                       psf[0:NP, a0 * D:a1 * D].rearrange("p (t d) -> p t d", d=D),
                                       ALU.mult, ALU.add).then_inc(rst_ready, 1)
            read_sorted(2)
            for step in range(NBANK + Z_LAG):
                if step == Z_LAG + 1:
                    decode(2)
                g = step - 2
                if 0 <= g < NBANK:
                    a0, a1 = groups[g]
                    y = y_sum[:, 0:a1 - a0, :]
                    dve.wait_ge(y_ps, g + 1)
                    V.tensor_tensor(y, ps[0:NP, 3, 0:(a1 - a0) * D].rearrange("p (t d) -> p t d", d=D),
                                    b2_sb[:, :, :].to_broadcast([NP, a1 - a0, D]), ALU.add).then_inc(y_used, 1)
                    dve.wait_ge(y_used, g + 1)
                    own(V.scalar_tensor_tensor(x_sb[:, a0:a1, :], y, 0.0, x_sb[:, a0:a1, :], ALU.max, ALU.add))
                    mean_var(a0, a1)
                g = step - 3
                if 0 <= g < NBANK:
                    norm(g + 1, *groups[g])
                g = step - Z_LAG
                if 0 <= g < NBANK:
                    for t in range(*groups[g]):
                        n = 2 * t
                        dve.wait_ge(z_ps, n + 1)
                        if n >= 4:
                            dve.wait_ge(z_stored[n % 4], 32 * (n // 4))
                        V.tensor_copy(z_stage[:, n % 4, :], z_half(n)).then_inc(z_even, 1)
            dve.wait_ge(wsT_ps, 1)
            V.tensor_copy(wsT[:, :], ps[:, 7, 0:D]).then_inc(wsT_ready, 1)
            for g, (a0, a1) in enumerate(groups):
                dve.wait_ge(self_ps, g + 1)
                V.tensor_tensor(x_sb[:, a0:a1, :], x_sb[:, a0:a1, :],
                                ps[0:NP, g, 0:(a1 - a0) * D].rearrange("p (t d) -> p t d", d=D), ALU.add).then_inc(self_used, 1)
            dve.wait_ge(self_used, NBANK)
            rounds(nc.vector, 2, node_hots, sort_batch)
            dve.wait_ge(nhot_used, RING[0] + sum(CHUNKS))
            for g, (a0, a1) in enumerate(groups):
                V.tensor_tensor(x_sb[:, a0:a1, :], x_sb[:, a0:a1, :],
                                psf[0:NP, a0 * D:a1 * D].rearrange("p (t d) -> p t d", d=D), ALU.add).then_inc(out_ready, 1)

        @block.tensor
        def _(pe):
            T = nc.tensor
            pe.sem_inc(nhot_used, RING[0])
            pe.sem_inc(batch_used, BATCH_BUFS)
            pe.wait_ge(consts_done, 1)

            def zero_bank(b):
                return T.matmul(ps[:, b, :], zeros_h[:, :], iota_h[:, :], start=True, stop=False, skip_group_check=True)

            def rank_sums(l):
                pe.wait_ge(count_ready, l + 1)
                T.matmul(pre_ps, before[0:EP, 0:EP], count[:, :], start=True, stop=True)
                T.matmul(tot_ps, ones[0:EP, :], count[:, :], start=True, stop=True).then_inc(prefix_done, 1)
                pe.wait_ge(tileof_ready, l + 1)
                for q in range(-(-CHUNKS[l] // P)):
                    w = min(P, CHUNKS[l] - q * P)
                    last = T.matmul(ps[0:1, 7, q * P:q * P + w], tile_of[:, q:q + 1], ident[:, 0:w], start=True, stop=True)
                last.then_inc(tilerow_done, 1)
                pe.wait_ge(toff_ready, l + 1)

            def sort_batch(s, batch, buf):
                for i in range(BATCH):
                    n = batch * BATCH + (COLS_BEFORE[s] + i + 1)
                    pe.wait_ge(chunk_ready, n)
                    for k, c0, c1, where in sort_regions[s]:
                        if k:
                            pe.wait_ge(val_ready, n)
                        val = place_val_b[:, buf, i, :] if k else place_val_a[:, buf, :, i]
                        last = T.matmul(where, val, chunk_hot[:, buf, i, c0:c1], start=False, stop=False,
                                        skip_group_check=True)
                last.then_inc(batch_used, 1)

            def add_up(s, g, r):
                _, offs = nc.values_load_multi_w_load_instructions(
                    tile_off[s][0:1, bass.ds(r * GROUPS + g, 1), 0:GROUP[s]].rearrange("p g i -> p (g i)"),
                    engines=[mybir.EngineType.PE], min_val=0, max_val=(TILES - 1) * D,
                    skip_runtime_bounds_check_because="tile_of is cut to the last tile")
                pe.wait_ge(got[s][g], r * (16 * GROUP[s]) + 16 * GROUP[s])
                for i in range(GROUP[s]):
                    k = g * GROUP[s] + i
                    pe.wait_ge(nhot_ready, r * RING[s] + (CHUNKS_BEFORE[s] + k + 1))
                    T.matmul(psf[0:NP, bass.ds(offs[i], D)], node_hot[:, k % HOTS[s], :], gathered[:, k, :],
                             start=False, stop=False, skip_group_check=True).then_inc(nhot_used, 1)

            rank_sums(0)
            for b in range(8):
                zero_bank(b)
            batches_ahead(nc.tensor, 0, sort_batch)
            for s in (1, 2):
                pe.wait_ge(decoded, s)
                rank_sums(s)
                zero_bank(7)
                batches_ahead(nc.tensor, s, sort_batch)
                rounds(nc.tensor, s - 1, add_up, sort_batch)
            pe.wait_ge(wrel_ready, 2 * N_BASES - 1)

            for step in range(NBANK + Z_LAG):
                g = step
                if 0 <= g < NBANK:
                    a0, a1 = groups[g]
                    pe.wait_ge(rst_ready, g + 1)
                    if g >= Z_LAG:
                        pe.wait_ge(h2T_ready, g - 5)
                    for t in range(a0, a1):
                        last = T.transpose(ps[:, g % 2, (t - a0) * NP:(t - a0 + 1) * NP], h_sb[:, t, :], ident[0:NP, 0:NP])
                    last.then_inc(featT_ps, 1)
                g = step - 2
                if 0 <= g < NBANK:
                    a0, a1 = groups[g]
                    pe.wait_ge(hid_ready, g + 1)
                    pe.wait_ge(rst_ready, min(NBANK, g + 4))
                    if g:
                        pe.wait_ge(y_used, g)
                    for t in range(a0, a1):
                        c = (t - a0) * D
                        last = T.matmul(ps[0:NP, 3, c:c + D], hidT[:, (t - a0) * NP:(t - a0 + 1) * NP], w2_sb[:, :],
                                        start=True, stop=True)
                    last.then_inc(y_ps, 1)
                g = step - 1
                if 0 <= g < NBANK:
                    w = (groups[g][1] - groups[g][0]) * NP
                    pe.wait_ge(rst_ready, min(NBANK, g + 3))
                    pe.wait_ge(ld_w, 96)
                    pe.wait_ge(featT_ready, g + 1)
                    if g:
                        pe.wait_ge(hid_ready, g)
                    T.matmul(ps[:, 2, 0:w], w1_sb[:, :], featT[:, 0:w], start=True, stop=True).then_inc(hid_ps, 1)
                g = step - 5
                if 0 <= g < NBANK:
                    a0, a1 = groups[g]
                    pe.wait_ge(h_ready, g + 2)
                    pe.wait_ge(featT_ready, min(NBANK, step))
                    if g >= 2:
                        pe.wait_ge(h2T_ready, g - 1)
                    for t in range(a0, a1):
                        last = T.transpose(ps[:, g % 2, (t - a0) * NP:(t - a0 + 1) * NP], h_sb[:, t, :], ident[0:NP, 0:NP])
                    last.then_inc(h2T_ps, 1)
                g = step - Z_LAG
                if 0 <= g < NBANK:
                    pe.wait_ge(h2T_ready, g + 1)
                    pe.wait_ge(sorted_read, 3)
                    for t in range(*groups[g]):
                        for half in range(2):
                            if t:
                                pe.wait_ge(z_odd if half else z_even, t)
                            for q in range(2):
                                last = T.matmul(z_half(half)[:, q * BANK:(q + 1) * BANK], h2T[:, t * NP:(t + 1) * NP],
                                                w_rel[:, half * 8 + q * 4:half * 8 + q * 4 + 4, :], start=True, stop=True)
                            last.then_inc(z_ps, 1)
            pe.wait_ge(z_even, TILES)
            pe.wait_ge(z_odd, TILES)
            pe.wait_ge(ld_w, 96)
            T.transpose(ps[:, 7, 0:D], ws_sb[:, :], ident[:, :]).then_inc(wsT_ps, 1)
            pe.wait_ge(wsT_ready, 1)
            for g, (a0, a1) in enumerate(groups):
                for t in range(a0, a1):
                    last = T.matmul(ps[0:NP, g, (t - a0) * D:(t - a0 + 1) * D], h2T[:, t * NP:(t + 1) * NP], wsT[:, :],
                                    start=True, stop=True)
                last.then_inc(self_ps, 1)
            pe.wait_ge(self_used, NBANK)
            for b in range(NBANK):
                zero_bank(b)
            rounds(nc.tensor, 2, add_up, sort_batch)


_INS = ["x", "src", "dst", "edge_type_16", "L0_gnn_eps", "L0_gnn_W1", "L0_gnn_b1", "L0_gnn_W2", "L0_gnn_b2",
        "L1_gnn_bases", "L1_gnn_coefficients", "L1_gnn_w_self"]


def kernel(**inputs):
    import concourse.bacc as _bacc
    from concourse.bass_utils import run_bass_kernel_spmd as _run

    nc = _bacc.Bacc("TRN2", target_bir_lowering=False, num_devices=1)
    arrays, args = {}, []
    for name in _INS:
        a = np.ascontiguousarray(inputs[name])
        arrays[f"in_{name}"] = a
        args.append(nc.dram_tensor(f"in_{name}", a.shape, mybir.dt.from_np(a.dtype), kind="ExternalInput").ap())
    out = nc.dram_tensor("out", (N_NODES, D), F32, kind="ExternalOutput").ap()
    build(nc, *args, out)
    r = _run(nc, [arrays], core_ids=[0])
    return r.results[0]["out"]
```

```python
import numpy as np
import concourse.bass as bass
from concourse import mybir
from contextlib import ExitStack

F32 = mybir.dt.float32
F16 = mybir.dt.float16
BF16 = mybir.dt.bfloat16
I32 = mybir.dt.int32
ALU = mybir.AluOpType
ACT = mybir.ActivationFunctionType
AX = mybir.AxisListType

N_NODES, N_EDGES, D, N_REL, N_BASES = 3125, 50000, 128, 16, 8
P = 128

TILES = 25
NP = N_NODES // TILES
DIV_MUL, DIV_SHIFT = 5243, 17

BUCKETS = -(-TILES // 2)
WIDE = 2 * NP

EC = 400
EP = N_EDGES // EC

SORTS = [(0, 0, 144, 3, 13), (0, 144, 256, 4, 11), (1, 0, 400, 5, 9)]
COLS = [cols for _, _, cols, _, _ in SORTS]
GROUP = [group for *_, group, _ in SORTS]
GROUPS = [groups for *_, groups in SORTS]
RING = [a * b for a, b in zip(GROUP, GROUPS)]
MOST = [(EP * cols + BUCKETS * (P - 1)) // P for cols in COLS]
ROUNDS = [-(-most // ring) for most, ring in zip(MOST, RING)]
CHUNKS = [rounds * ring for rounds, ring in zip(ROUNDS, RING)]
CHUNKS_BEFORE = [sum(CHUNKS[:s]) for s in range(3)]
COLS_BEFORE = [sum(COLS[:s]) for s in range(3)]
WIDEST = max(CHUNKS)
HOTS = [13, 22, 9]
assert all(ring % hots == 0 for ring, hots in zip(RING, HOTS))
GROW = [-(-group // 4) * 4 for group in GROUP]

BATCH = 8
BATCH_BUFS = 2
BESIDE_ROUNDS = [0, 3, 6]
ALONE_ROUND = [0, 0, 3]
PER_ROUND = [0] + [COLS[s] // (BATCH * BESIDE_ROUNDS[s]) // BATCH_BUFS * BATCH_BUFS for s in (1, 2)]
ALONE = [COLS[s] // BATCH - BESIDE_ROUNDS[s] * PER_ROUND[s] for s in range(3)]
BATCHES_BEFORE = [c // BATCH for c in COLS_BEFORE]
assert all(n % BATCH_BUFS == 0 for n in PER_ROUND) and all(c % BATCH == 0 for c in COLS)

BIG = 1000.0

SPLITS = 3
BANK = 512
BT = BANK // D
NBANK = -(-TILES // BT)
SPLIT = 112
EPS = 1e-5
Z_BUFS = 4
Z_HALF = N_REL * D // 2
ACT_FIRST = 6
BASES_FIRST = 4
Z_LAG = 4


def build(nc, x, src, dst, etype, eps, W1, b1, W2, b2, bases, coef, w_self, out):
    ctx = ExitStack()
    with ctx:
        def sb(name, shape, dt):
            return ctx.enter_context(nc.sbuf_tensor(name, shape, dt))

        def sem(name):
            return ctx.enter_context(nc.semaphore(name))

        h_table = nc.dram_tensor("h_table", [N_NODES, SPLITS * D], BF16).ap()
        z_table = nc.dram_tensor("z_table", [N_NODES * N_REL, D], F32).ap()

        iota_i = sb("iota_i", [P, BANK], I32)
        pidx_i = sb("pidx_i", [P, 4], I32)
        iota_f = sb("iota_f", [P, BANK], F32)
        iota_h = sb("iota_h", [P, BANK], F16)
        iota_run = sb("iota_run", [P, P, BATCH], F16)
        pidx = sb("pidx", [P, 4], F32)
        ident = sb("ident", [P, P], F32)
        before = sb("before", [P, P], F32)
        ones = sb("ones", [P, P], F32)
        zeros_h = sb("zeros_h", [P, P], F16)
        w1_sb = sb("w1_sb", [D, D], F32)
        w2_sb = sb("w2_sb", [D, D], F32)
        ws_sb = sb("ws_sb", [D, D], F32)
        wsT = sb("wsT", [D, D], F32)
        b1_sb = sb("b1_sb", [D, 1], F32)
        b2_sb = sb("b2_sb", [NP, 1, D], F32)
        eps1 = sb("eps1", [P, 1], F32)
        ident_eps = sb("ident_eps", [P, P], F32)
        coef_sb = sb("coef_sb", [P, N_REL * N_BASES], F32)
        bases_sb = sb("bases_sb", [D, N_BASES, D], F32)
        w_rel = sb("w_rel", [D, N_REL, D], F32)
        ends_i = [sb("dst_i", [EP, EC], I32), sb("src_i", [EP, EC], I32)]
        dst_i, src_i = ends_i
        type_i = sb("type_i", [EP, EC], I32)
        t0 = sb("t0", [EP, EC], I32)
        t1 = sb("t1", [EP, EC], I32)
        low_i = sb("low_i", [EP, EC], I32)
        bucket_h = sb("bucket_h", [EP, EC], F16)
        row_i = sb("row_i", [EP, EC], I32)
        scratch = sb("scratch", [P, BUCKETS * EC // 2], F32)
        member_flat = scratch[0:EP, :].bitcast(BF16)
        s0, s1, s2 = (scratch[:, i * WIDEST:(i + 1) * WIDEST].bitcast(I32) for i in range(3))
        pad_f = scratch[:, 3 * WIDEST:4 * WIDEST]
        spare = sb("spare", [P, Z_BUFS * Z_HALF + TILES * NP + BT * NP + BT * D], F32)
        spot_i = sb("spot_i", [EP, EC], I32)
        chunk_f = [sb(f"chunk_f{l}", [EP, EC], F32) for l in range(2)]
        place_h = [sb(f"place_h{l}", [EP, EC], F16) for l in range(2)]
        code_a = [sb(f"code_a{l}", [EP, EC], F16) for l in range(2)]
        code_b = [sb(f"code_b{l}", [EP, EC], F32) for l in range(2)]
        count = sb("count", [EP, BUCKETS], F32)
        lower = sb("lower", [EP, BUCKETS], F32)
        adjust = sb("adjust", [EP, BUCKETS], F32)
        need_i = sb("need_i", [P, BUCKETS], I32)
        need_f = sb("need_f", [P, BUCKETS], F32)
        upto = sb("upto", [P, BUCKETS], F32)
        le_scr = sb("le_scr", [P, BUCKETS], F32)
        bucket_of = sb("bucket_of", [P, 4], F32)
        bucket_off = [sb(f"bucket_off{s}", [1, ROUNDS[s] * GROUPS[s], GROW[s]], I32) for s in range(3)]
        chunk_hot = sb("chunk_hot", [EP, BATCH_BUFS, BATCH, WIDEST], F16)
        place_hot = sb("place_hot", [EP, BATCH_BUFS, P, BATCH], F16)
        place_val_a = sb("place_val_a", [EP, BATCH_BUFS, P, BATCH], F16)
        place_val_b = sb("place_val_b", [EP, BATCH_BUFS, BATCH, P], F16)
        row_of = [sb(f"row_of{s}", [P, CHUNKS[s]], I32) for s in range(3)]
        key_of = [sb(f"key_of{s}", [P, CHUNKS[s]], F32) for s in range(3)]
        row_stage = [sb(f"row_stage{s}", [P, GROUPS[s], GROUP[s]], I32) for s in range(3)]
        gathered = sb("gathered", [P, RING[1] * SPLITS * D // 2], F32)
        gathered_of = [gathered[:, :].bitcast(BF16).rearrange("p (k j d) -> p k j d", j=SPLITS, d=D)] * 2 + [
            gathered[:, 0:RING[2] * D].rearrange("p (k d) -> p k d", d=D)]
        node_hot = sb("node_hot", [P, max(HOTS[1] // 2, HOTS[2]) * WIDE], F32)
        node_hot_of = [node_hot[:, :].bitcast(BF16).rearrange("p (k n) -> p k n", n=WIDE)] * 2 + [
            node_hot[:, 0:HOTS[2] * WIDE].rearrange("p (k n) -> p k n", n=WIDE)]
        x_sb = sb("x_sb", [NP, TILES, D], F32)
        h_sb = sb("h_sb", [NP, TILES, D], F32)
        stats = sb("stats", [NP, TILES, 6], F32)
        mv = sb("mv", [NP, TILES, 2], F32)
        sd = sb("sd", [NP, TILES], F32)
        rstd = sb("rstd", [NP, TILES], F32)
        shift = sb("shift", [NP, TILES], F32)
        row_sum = sb("row_sum", [NP, TILES], F32)
        square_sum = sb("square_sum", [NP, TILES], F32)
        neg_mean = sb("neg_mean", [NP, TILES, 1], F32)
        rstd0 = sb("rstd0", [NP, TILES, 1], F32)
        epsc = sb("epsc", [P, 1], F32)
        w_part = gathered[:, 0:N_REL * D].rearrange("p (r d) -> p r d", d=D)
        h_parts = gathered[0:NP, N_REL * D:N_REL * D + TILES * SPLITS * D // 2].bitcast(BF16).rearrange(
            "p (t j d) -> p t j d", j=SPLITS, d=D)
        featT = gathered[:, N_REL * D:N_REL * D + TILES * NP]
        rest = spare[0:NP, BUCKETS * COLS[0]:BUCKETS * COLS[0] + TILES * D].rearrange("p (t d) -> p t d", d=D)
        w_part_dve = spare[:, BUCKETS * EC:BUCKETS * EC + N_REL * D].rearrange("p (r d) -> p r d", d=D)
        z_stage = spare[0:NP, 0:Z_BUFS * Z_HALF].rearrange("p (s n) -> p s n", s=Z_BUFS)
        free = Z_BUFS * Z_HALF
        h2T = spare[:, free:free + TILES * NP]
        free += TILES * NP
        hidT = spare[:, free:free + BT * NP]
        free += BT * NP
        y_sum = spare[0:NP, free:free + BT * D].rearrange("p (t d) -> p t d", d=D)

        ps = ctx.enter_context(nc.psum_tensor("ps", [P, 8, BANK], F32))
        psf = ps[:, :, :].rearrange("p b c -> p (b c)")
        LASTB = NBANK - 1
        USED = NP
        pre_ps = ps[0:EP, 7, 448:448 + BUCKETS]
        tot_ps = ps[:, 7, 480:480 + BUCKETS]
        room = BANK - USED
        sort_regions = []
        for w in CHUNKS:
            parts = [(0, 0, w, ps[:, 7, 0:w]), (1, 0, min(w, room), ps[:, LASTB, USED:USED + min(w, room)])]
            if w > room:
                parts.append((1, room, w, ps[:, 7, w:w + w - room]))
            sort_regions.append(parts)

        ld_edge, ld_eps, ld_type = sem("ld_edge"), sem("ld_eps"), sem("ld_type")
        ld_x, ld_w, ld_c = sem("ld_x"), sem("ld_w"), sem("ld_c")
        iota_done = sem("iota_done")
        consts_done = sem("consts_done")
        v = sem("v")
        a = sem("a")
        count_ready = sem("count_ready")
        prefix_done = sem("prefix_done")
        bucket_of_ready = sem("bucket_of_ready")
        bucket_row_done = sem("bucket_row_done")
        bucket_off_ready = sem("bucket_off_ready")
        place_ready = sem("place_ready")
        batch_ready = sem("batch_ready")
        val_ready = sem("val_ready")
        batch_used = sem("batch_used")
        sorted_read = sem("sorted_read")
        decoded, keys_decoded = sem("decoded"), sem("keys_decoded")
        staged = [[sem(f"staged{l}_{g}") for g in range(GROUPS[l])] for l in range(3)]
        begun = sem("begun")
        got = [[sem(f"got{l}_{g}") for g in range(GROUPS[l])] for l in range(3)]
        nhot_ready = sem("nhot_ready")
        nhot_used = sem("nhot_used")
        var_ready = sem("var_ready")
        sd_ready = sem("sd_ready")
        rstd0_ready = sem("rstd0_ready")
        centred = sem("centred")
        parts_ready = sem("parts_ready")
        rest_ready = sem("rest_ready")
        eps_ready = sem("eps_ready")
        norm_ready = sem("norm_ready")
        h_ready = sem("h_ready")
        h_stored = sem("h_stored")
        sums_read = sem("sums_read")
        hid_ps = sem("hid_ps")
        hid_ready = sem("hid_ready")
        y_ps = sem("y_ps")
        y_used = sem("y_used")
        h2T_ps = sem("h2T_ps")
        h2T_ready = sem("h2T_ready")
        wsT_ps = sem("wsT_ps")
        wsT_ready = sem("wsT_ready")
        wrel_ready = sem("wrel_ready")
        z_ps = sem("z_ps")
        z_even, z_odd = sem("z_even"), sem("z_odd")
        z_stored = [sem(f"z_stored{s}") for s in range(Z_BUFS)]
        out_ready = sem("out_ready")
        out_stored = sem("out_stored")

        x_rows = x.rearrange("(p t) d -> p t d", t=TILES)
        h_rows = h_table.rearrange("(p t) (j d) -> p t j d", t=TILES, d=D)
        z_rows = z_table.rearrange("(p t r) d -> p t (r d)", t=TILES, r=N_REL)
        out_rows = out.rearrange("(p t) d -> p t d", t=TILES)
        PARTS = ((0, SPLIT), (SPLIT, NP))
        groups = [(BT * g, min(TILES, BT * (g + 1))) for g in range(NBANK)]

        def z_half(n):
            return psf[0:NP, (4 + 2 * (n % 2)) * BANK:(6 + 2 * (n % 2)) * BANK]

        def batches_alone(engine, s, sort_batch, first, last):
            turns = (last - first) // BATCH_BUFS
            if turns:
                with engine.Fori(0, turns) as r:
                    for b in range(BATCH_BUFS):
                        sort_batch(s, r * BATCH_BUFS + (first + b), (BATCHES_BEFORE[s] + first + b) % BATCH_BUFS)
            for b in range(first + turns * BATCH_BUFS, last):
                sort_batch(s, b, (BATCHES_BEFORE[s] + b) % BATCH_BUFS)

        def rounds_beside(engine, s, group_work, sort_batch, between=None):
            mid, per_round, alone = ALONE_ROUND[s + 1], PER_ROUND[s + 1], ALONE[s + 1]
            for r0, r1, taken in ((0, mid, 0), (mid, BESIDE_ROUNDS[s + 1], alone)):
                if r0 == r1:
                    continue
                if taken:
                    batches_alone(engine, s + 1, sort_batch, mid * per_round, mid * per_round + alone)
                    if between:
                        between()
                with engine.Fori(r0, r1) as r:
                    for g in range(GROUPS[s]):
                        group_work(s, g, r)
                        b0, b1 = (min(n, GROUPS[s] - 1) * per_round // (GROUPS[s] - 1) for n in (g, g + 1))
                        for b in range(b0, b1):
                            sort_batch(s + 1, r * per_round + (taken + b), (BATCHES_BEFORE[s + 1] + taken + b) % BATCH_BUFS)

        def rounds_rest(engine, s, group_work):
            beside = (BESIDE_ROUNDS + [0])[s + 1]
            if beside < ROUNDS[s]:
                with engine.Fori(beside, ROUNDS[s]) as r:
                    for g in range(GROUPS[s]):
                        group_work(s, g, r)

        block = ctx.enter_context(nc.Block())

        def stage_rows(sp, s):
            sp.wait_ge(decoded, s + 1)
            if s:
                for g in range(GROUPS[s]):
                    sp.wait_ge(nhot_used, CHUNKS_BEFORE[s] - RING[s - 1] + min((g + 1) * GROUP[s], RING[s - 1]) + RING[0])
                    sp.dma_start(row_stage[s][:, g, :],
                                 row_of[s][:, g * GROUP[s]:(g + 1) * GROUP[s]]).then_inc(staged[s][g], 16)
            with nc.sync.Fori(min(s, 1), ROUNDS[s]) as r:
                for g in range(GROUPS[s]):
                    sp.wait_ge(nhot_used, r * RING[s] + (CHUNKS_BEFORE[s] + (g + 1) * GROUP[s] + RING[0] - RING[s]))
                    sp.dma_start(row_stage[s][:, g, :],
                                 row_of[s][:, bass.ds(r * RING[s] + g * GROUP[s], GROUP[s])]).then_inc(staged[s][g], 16)

        @block.sync
        def _(sp):
            for t, d in ((dst_i, dst), (src_i, src)):
                sp.dma_start(t[:, :], d.rearrange("(p c) -> p c", c=EC)).then_inc(ld_edge, 16)
            for p0, p1 in PARTS:
                sp.dma_start(x_sb[p0:p1, :, :], x_rows[p0:p1, :, :]).then_inc(ld_x, 16)
            sp.dma_start(coef_sb[:, :], coef.rearrange("(o r) b -> o (r b)", o=1).to_broadcast([P, N_REL * N_BASES])).then_inc(ld_c, 16)
            sp.dma_start(bases_sb[:, :, :], bases.rearrange("b i o -> i b o")).then_inc(ld_c, 16)
            sp.dma_start(eps1[:, :], eps.rearrange("(o d) -> o d", o=1).to_broadcast([P, 1])).then_inc(ld_eps, 16)
            sp.dma_start(type_i[:, :], etype.rearrange("(p c) -> p c", c=EC)).then_inc(ld_type, 16)
            sp.dma_start(w1_sb[:, :], W1).then_inc(ld_w, 16)
            sp.dma_start(w2_sb[:, :], W2).then_inc(ld_w, 16)
            sp.dma_start(ws_sb[:, :], w_self).then_inc(ld_w, 16)
            sp.dma_start(b1_sb[:, :], b1.rearrange("(p o) -> p o", o=1)).then_inc(ld_w, 16)
            sp.dma_start(b2_sb[:, 0, :], b2.rearrange("(o d) -> o d", o=1).to_broadcast([NP, D])).then_inc(ld_w, 16)
            sp.wait_ge(parts_ready, SPLITS)
            for p0, p1 in PARTS:
                sp.dma_start(h_rows[p0:p1, :, :, :], h_parts[p0:p1, :, :, :]).then_inc(h_stored, 16)
            stage_rows(sp, 0)
            stage_rows(sp, 1)
            for t in range(TILES):
                for half in range(2):
                    slot = (2 * t + half) % Z_BUFS
                    if half == 0:
                        sp.wait_ge(z_even, t + 1)
                    else:
                        sp.wait_ge(z_odd, t + 1)
                    for p0, p1 in PARTS:
                        sp.dma_start(z_rows[p0:p1, t, half * Z_HALF:(half + 1) * Z_HALF],
                                     z_stage[p0:p1, slot, :]).then_inc(z_stored[slot], 16)
            stage_rows(sp, 2)
            for g in range(NBANK):
                sp.wait_ge(out_ready, g + 1)
                a0, a1 = groups[g]
                for p0, p1 in PARTS:
                    sp.dma_start(out_rows[p0:p1, a0:a1, :], x_sb[p0:p1, a0:a1, :]).then_inc(out_stored, 16)
            sp.wait_ge(out_stored, 32 * NBANK)

        @block.gpsimd
        def _(pool):
            pool.iota(iota_i[:, :], [[1, BANK]], base=0, channel_multiplier=0).then_inc(iota_done, 1)
            pool.iota(pidx_i[:, :], [[P, 4]], base=0, channel_multiplier=1).then_inc(iota_done, 1)

            def add_bases(b0, b1):
                for b in range(b0, b1):
                    base = bases_sb[:, b:b + 1, :].to_broadcast([D, N_REL, D])
                    share = coef_sb[:, :].rearrange("p (r b) -> p r b", b=N_BASES)[:, :, b:b + 1].to_broadcast([D, N_REL, D])
                    pool.tensor_tensor((w_part if b else w_rel)[:, :, :], base, share, ALU.mult).then_inc(wrel_ready, 1)
                    if b:
                        pool.wait_ge(wrel_ready, 2 * b)
                        pool.tensor_tensor(w_rel[:, :, :], w_rel[:, :, :], w_part[:, :, :], ALU.add).then_inc(wrel_ready, 1)
                        pool.wait_ge(wrel_ready, 2 * b + 1)

            pool.wait_ge(ld_c, 32)
            add_bases(0, 3)
            pool.wait_ge(rstd0_ready, 1)
            pool.tensor_tensor(h_sb[:, :, :], x_sb[:, :, :], neg_mean[:, :, :].to_broadcast([NP, TILES, D]),
                               ALU.add).then_inc(centred, 1)
            pool.wait_ge(centred, 1)
            pool.tensor_tensor(h_sb[:, :, :], h_sb[:, :, :], rstd0[:, :, :].to_broadcast([NP, TILES, D]),
                               ALU.mult).then_inc(centred, 1)
            pool.wait_ge(parts_ready, 1)
            pool.tensor_tensor(rest[:, :, :], h_sb[:, :, :], h_parts[:, :, 0, :], ALU.subtract).then_inc(rest_ready, 1)
            pool.wait_ge(rest_ready, 1)
            pool.tensor_copy(h_parts[:, :, 1, :], rest[:, :, :]).then_inc(parts_ready, 1)
            pool.wait_ge(parts_ready, 2)
            pool.tensor_tensor(h_parts[:, :, 2, :], rest[:, :, :], h_parts[:, :, 1, :], ALU.subtract).then_inc(parts_ready, 1)
            add_bases(3, BASES_FIRST)
            for s in range(3):
                table = h_table if s < 2 else z_table
                if s == 2:
                    for q in range(Z_BUFS - 1):
                        pool.wait_ge(z_stored[q], 32 * (-(-(2 * TILES - q) // Z_BUFS)))
                with nc.gpsimd.Fori(0, ROUNDS[s]) as r:
                    for g in range(GROUPS[s]):
                        if s < 2:
                            pool.wait_ge(h_stored, 32)
                        else:
                            pool.wait_ge(z_stored[-1], 32 * (2 * TILES // Z_BUFS))
                        pool.wait_ge(staged[s][g], r * 16 + 16)
                        pool.sem_inc(begun, 1)
                        for i in range(GROUP[s]):
                            place = gathered_of[s][:, g * GROUP[s] + i]
                            pool.indirect_dma_start(
                                place.rearrange("p j d -> p (j d)") if s < 2 else place, None, table,
                                bass.IndirectOffsetOnAxis(ap=row_stage[s][:, g, i:i + 1], axis=0)).then_inc(got[s][g], 16)

        @block.scalar
        def _(act):
            done = 0

            def own(ins):
                nonlocal done
                ins.then_inc(a, 1)
                done += 1
                act.wait_ge(a, done)

            act.wait_ge(consts_done, 1)
            act.wait_ge(ld_x, 32)
            for t in range(TILES):
                last = nc.scalar.activation(h_sb[:, t, :], x_sb[:, t, :], ACT.Copy, accum_out=row_sum[:, t:t + 1])
            own(last)
            own(nc.scalar.activation(neg_mean[:, :, 0], row_sum[:, :], ACT.Copy, scale=-1.0 / D))
            for t in range(TILES):
                last = nc.scalar.activation(h_sb[:, t, :], x_sb[:, t, :], ACT.Square, bias=neg_mean[:, t, :],
                                            accum_out=square_sum[:, t:t + 1])
            own(last)
            nc.scalar.activation(sd[:, :], square_sum[:, :], ACT.Sqrt, bias=epsc[0:NP, :], scale=1.0 / D).then_inc(sd_ready, 1)

            def sort_batch(s, batch, buf):
                l, c0, *_ = SORTS[s]
                act.wait_ge(place_ready, batch + (BATCHES_BEFORE[s] + 1))
                for i in range(BATCH):
                    nc.scalar.activation(place_val_b[:, buf, i, :], place_hot[:, buf, :, i], ACT.Copy,
                                         scale=code_b[l][:, bass.ds(batch * BATCH + (c0 + i), 1)]).then_inc(val_ready, 1)

            for b in range(ACT_FIRST):
                sort_batch(0, b, b % BATCH_BUFS)
            act.wait_ge(centred, 2)
            nc.scalar.activation(h_sb[:, :, :], h_sb[:, :, :], ACT.Relu).then_inc(h_ready, 1)
            act.wait_ge(h_ready, 1)
            nc.scalar.copy(h_parts[:, :, 0, :], h_sb[:, :, :]).then_inc(parts_ready, 1)
            batches_alone(nc.scalar, 0, sort_batch, ACT_FIRST, ALONE[0])
            for s in (1, 2):
                batches_alone(nc.scalar, s, sort_batch, 0, COLS[s] // BATCH)

            def z_odd_copies(tiles):
                for t in tiles:
                    n = 2 * t + 1
                    act.wait_ge(z_ps, n + 1)
                    if n >= Z_BUFS:
                        act.wait_ge(z_stored[n % Z_BUFS], 32 * (n // Z_BUFS))
                    nc.scalar.copy(z_stage[:, n % Z_BUFS, :], z_half(n)).then_inc(z_odd, 1)

            for step in range(NBANK + Z_LAG):
                z_tiles = range(*groups[step - Z_LAG]) if step >= Z_LAG else ()
                g = step
                if 0 <= g < NBANK:
                    act.wait_ge(hid_ps, g + 1)
                    w = (groups[g][1] - groups[g][0]) * NP
                    nc.scalar.activation(hidT[:, 0:w], ps[:, 2, 0:w], ACT.Relu, bias=b1_sb[:, :]).then_inc(hid_ready, 1)
                g = step - 3
                if 0 <= g < NBANK:
                    a0, a1 = groups[g]
                    act.wait_ge(h2T_ps, g + 1)
                    nc.scalar.copy(h2T[:, a0 * NP:a1 * NP], ps[:, g % 2, 0:(a1 - a0) * NP]).then_inc(h2T_ready, 1)
                z_odd_copies(z_tiles[:2])
                g = step - 2
                if 0 <= g < NBANK:
                    act.wait_ge(norm_ready, g + 1)
                    for t in range(*groups[g]):
                        last = nc.scalar.activation(h_sb[:, t, :], x_sb[:, t, :], ACT.Relu, bias=shift[:, t:t + 1],
                                                    scale=rstd[:, t:t + 1])
                    last.then_inc(h_ready, 1)
                z_odd_copies(z_tiles[2:])
                g = step - 1
                if 0 <= g < NBANK:
                    a0, a1 = groups[g]
                    act.wait_ge(var_ready, g + 1)
                    nc.scalar.activation(sd[:, a0:a1], mv[:, a0:a1, 1], ACT.Sqrt, bias=epsc[0:NP, :]).then_inc(sd_ready, 1)

        @block.vector
        def _(dve):
            done = 0

            def own(ins):
                nonlocal done
                ins.then_inc(v, 1)
                done += 1
                dve.wait_ge(v, done)

            V = nc.vector
            dve.wait_ge(iota_done, 2)
            V.tensor_copy(iota_f[:, :], iota_i[:, :])
            V.tensor_copy(iota_h[:, :], iota_i[:, :])
            V.memset(ones[:, :], 1.0)
            V.memset(zeros_h[:, :], 0.0)
            V.memset(epsc[:, :], EPS)
            V.tensor_copy(iota_run[:, :, :],
                          iota_i[:, 0:P].rearrange("p (v o) -> p v o", o=1).to_broadcast([P, P, BATCH]))
            own(V.tensor_copy(pidx[:, :], pidx_i[:, :]))
            V.tensor_scalar(ident[:, :], iota_f[:, 0:P], pidx[:, 0:1], None, ALU.is_equal)
            V.tensor_scalar(before[:, :], iota_f[:, 0:P], pidx[:, 0:1], None, ALU.is_gt).then_inc(consts_done, 1)

            def mean_var(a0, a1):
                for t in range(a0, a1):
                    last = V.bn_stats(stats[:, t, :], x_sb[:, t, :])
                own(last)
                for t in range(a0, a1):
                    last = V.bn_aggr(mv[:, t, :], stats[:, t, :])
                last.then_inc(var_ready, 1)

            def rank_views(s):
                l, c0, cols, *_ = SORTS[s]
                cs = slice(c0, c0 + cols)
                row = (src_i if l == 0 else row_i)[:, cs]
                member_f = member_flat[:, 0:BUCKETS * cols]
                running_f = spare[0:EP, 0:BUCKETS * cols]
                return l, cs, row, low_i[:, cs], t0[:, cs], t1[:, cs], member_f, running_f

            def rank_count(s):
                l, cs, row, low, scr0, scr1, member_f, running_f = rank_views(s)
                cols = COLS[s]
                key = ends_i[l][:, cs]
                member = member_f.rearrange("p (b c) -> p b c", c=cols)
                running = running_f.rearrange("p (b c) -> p b c", c=cols)
                if l == 1:
                    dve.wait_ge(ld_type, 16)
                    own(V.scalar_tensor_tensor(row, dst_i[:, cs], float(N_REL), type_i[:, cs], ALU.mult, ALU.add))
                own(V.tensor_scalar(scr0, key, float(DIV_MUL), None, ALU.mult))
                own(V.tensor_scalar(low, scr0, DIV_SHIFT, None, ALU.logical_shift_right))
                own(V.scalar_tensor_tensor(scr0, low, -float(TILES), key, ALU.mult, ALU.add))
                V.tensor_scalar(scr1, scr0, 1, None, ALU.bitwise_and)
                own(V.tensor_scalar(scr0, scr0, 1, None, ALU.logical_shift_right))
                own(V.scalar_tensor_tensor(low, scr1, float(NP), low, ALU.mult, ALU.add))
                own(V.tensor_copy(bucket_h[:, cs], scr0))
                for b in range(BUCKETS):
                    last = V.tensor_scalar(member[:, b, :], bucket_h[:, cs], float(b), None, ALU.is_equal)
                own(last)
                own(V.tensor_tensor_scan(running_f, member_f, member_f, 0.0, ALU.add, ALU.bypass))
                V.tensor_copy(count[:, 0:1], running[:, 0, cols - 1:cols])
                V.tensor_tensor(count[:, 1:BUCKETS], running[:, 1:BUCKETS, cols - 1], running[:, 0:BUCKETS - 1, cols - 1],
                                ALU.subtract).then_inc(count_ready, 1)
                dve.wait_ge(prefix_done, s + 1)
                dve.wait_ge(count_ready, s + 1)
                V.tensor_copy(lower[:, :], pre_ps)
                own(V.tensor_scalar(need_i[:, :], tot_ps, float(P - 1), None, ALU.add))
                own(V.tensor_scalar(need_i[:, :], need_i[:, :], 7, None, ALU.logical_shift_right))
                own(V.tensor_copy(need_f[:, :], need_i[:, :]))
                own(V.tensor_tensor_scan(upto[:, :], need_f[:, :], need_f[:, :], 0.0, ALU.add, ALU.bypass))
                for q in range(4):
                    own(V.tensor_scalar(le_scr[:, :], upto[:, :], pidx[:, q:q + 1], 0.0, ALU.is_le, ALU.add,
                                        accum_out=bucket_of[:, q:q + 1]))
                V.tensor_scalar(bucket_of[:, :], bucket_of[:, :], float(BUCKETS - 1), float(2 * D), ALU.min, ALU.mult).then_inc(bucket_of_ready, 1)
                own(V.tensor_tensor(need_f[:, :], upto[:, :], need_f[:, :], ALU.subtract))
                own(V.scalar_tensor_tensor(adjust[:, :], need_f[0:EP, :], float(P), lower[:, :], ALU.mult, ALU.add))
                own(V.scalar_tensor_tensor(adjust[:, :], adjust[:, :], -1.0, count[:, :], ALU.add, ALU.add))
                own(V.tensor_tensor(adjust[:, :], adjust[:, :], running[:, :, cols - 1], ALU.subtract))
                dve.wait_ge(bucket_row_done, s + 1)
                V.tensor_copy(bucket_off[s][:, :, 0:GROUP[s]],
                              ps[0:1, 7, 0:CHUNKS[s]].rearrange("p (g i) -> p g i", i=GROUP[s])).then_inc(bucket_off_ready, 1)

            def rank_place(s):
                l, cs, row, low, scr0, scr1, member_f, running_f = rank_views(s)
                spot = spot_i[:, cs]
                member = member_f.rearrange("p (b c) -> p b c", c=COLS[s])
                running = running_f.rearrange("p (b c) -> p b c", c=COLS[s])
                for b in range(BUCKETS):
                    last = V.scalar_tensor_tensor(running[:, b, :], running[:, b, :], adjust[:, b:b + 1], member[:, b, :],
                                                  ALU.add, ALU.mult)
                own(last)
                own(V.tensor_reduce(chunk_f[l][:, cs], running.rearrange("p b c -> p c b"), AX.X, ALU.add))
                own(V.tensor_copy(spot, chunk_f[l][:, cs]))
                V.tensor_scalar(scr0, spot, 7, None, ALU.logical_shift_right)
                own(V.tensor_scalar(scr1, spot, P - 1, None, ALU.bitwise_and))
                V.tensor_copy(chunk_f[l][:, cs], scr0)
                own(V.tensor_copy(place_h[l][:, cs], scr1))
                V.tensor_scalar(scr0, row, 8, 4, ALU.logical_shift_right, ALU.logical_shift_left)
                own(V.tensor_scalar(scr1, low, 4, None, ALU.logical_shift_right))
                own(V.scalar_tensor_tensor(scr0, scr0, 1.0, scr1, ALU.add, ALU.add))
                own(V.tensor_scalar(scr1, scr0, 2048.0, -4096.0, ALU.is_gt, ALU.mult))
                own(V.tensor_tensor(code_a[l][:, cs], scr0, scr1, ALU.add))
                V.tensor_scalar(scr0, row, 255, 4, ALU.bitwise_and, ALU.logical_shift_left)
                own(V.tensor_scalar(scr1, low, 15, None, ALU.bitwise_and))
                own(V.scalar_tensor_tensor(code_b[l][:, cs], scr0, -2048.0, scr1, ALU.add, ALU.add))

            def sort_batch(s, batch, buf):
                l, c0, *_ = SORTS[s]
                dve.wait_ge(batch_used, batch + (BATCHES_BEFORE[s] + 1))
                run = bass.ds(batch * BATCH + c0, BATCH)
                V.tensor_tensor(place_hot[:, buf, :, :], iota_run[0:EP, :, :],
                                place_h[l][:, run].rearrange("p (o c) -> p o c", o=1).to_broadcast([EP, P, BATCH]),
                                ALU.is_equal).then_inc(place_ready, 1)
                for i in range(BATCH):
                    V.tensor_scalar(chunk_hot[:, buf, i, 0:CHUNKS[s]], iota_h[0:EP, 0:CHUNKS[s]],
                                    chunk_f[l][:, bass.ds(batch * BATCH + (c0 + i), 1)], None, ALU.is_equal)
                dve.wait_ge(place_ready, batch + (BATCHES_BEFORE[s] + 1))
                V.tensor_tensor(place_val_a[:, buf, :, :], place_hot[:, buf, :, :],
                                code_a[l][:, run].rearrange("p (o c) -> p o c", o=1).to_broadcast([EP, P, BATCH]),
                                ALU.mult).then_inc(batch_ready, 1)

            def read_sorted(s):
                dve.wait_ge(batch_used, BATCH_BUFS + BATCHES_BEFORE[s] + COLS[s] // BATCH)
                if s:
                    dve.wait_ge(nhot_used, RING[0] + CHUNKS_BEFORE[s - 1] + BESIDE_ROUNDS[s] * RING[s - 1])
                w = CHUNKS[s]
                pa = ps[:, 7, 0:w]
                V.tensor_scalar(s0[:, 0:w], pa, -1.0, None, ALU.add)
                V.tensor_scalar(s2[:, 0:w], pa, 0.0, 4096.0, ALU.is_lt, ALU.mult)
                last = V.tensor_scalar(pad_f[:, 0:w], pa, 0.0, BIG, ALU.is_equal, ALU.mult)
                for k, c0, c1, where in sort_regions[s]:
                    if k == 1:
                        last = V.tensor_scalar(s1[:, c0:c1], where, 2048.0, None, ALU.add)
                last.then_inc(sorted_read, 1)
                dve.wait_ge(sorted_read, s + 1)
                if s < 2:
                    V.memset(ps[:, LASTB, USED:BANK], 0.0)

            def decode_rows(s):
                w = CHUNKS[s]
                own(V.tensor_tensor(s0[:, 0:w], s0[:, 0:w], s2[:, 0:w], ALU.add))
                own(V.tensor_scalar(s0[:, 0:w], s0[:, 0:w], 0.0, None, ALU.max))
                own(V.tensor_scalar(s2[:, 0:w], s0[:, 0:w], 4, 8, ALU.logical_shift_right, ALU.logical_shift_left))
                own(V.tensor_scalar(row_of[s][:, :], s1[:, 0:w], 4, None, ALU.logical_shift_right))
                V.tensor_tensor(row_of[s][:, :], row_of[s][:, :], s2[:, 0:w], ALU.add).then_inc(decoded, 1)
                dve.wait_ge(decoded, s + 1)

            def decode_keys(s):
                w = CHUNKS[s]
                own(V.tensor_scalar(s0[:, 0:w], s0[:, 0:w], 15, 4, ALU.bitwise_and, ALU.logical_shift_left))
                own(V.tensor_scalar(s1[:, 0:w], s1[:, 0:w], 15, None, ALU.bitwise_and))
                own(V.tensor_tensor(pad_f[:, 0:w], pad_f[:, 0:w], s0[:, 0:w], ALU.add))
                V.tensor_tensor(key_of[s][:, :], pad_f[:, 0:w], s1[:, 0:w], ALU.add).then_inc(keys_decoded, 1)
                dve.wait_ge(keys_decoded, s + 1)

            def node_hots(s, g, r):
                for i in range(GROUP[s]):
                    k = g * GROUP[s] + i
                    dve.wait_ge(nhot_used, r * RING[s] + (CHUNKS_BEFORE[s] + k + 1 + RING[0] - HOTS[s]))
                    V.tensor_scalar(node_hot_of[s][:, k % HOTS[s], :], (iota_h if s < 2 else iota_f)[:, 0:WIDE],
                                    key_of[s][:, bass.ds(r * RING[s] + k, 1)],
                                    None, ALU.is_equal).then_inc(nhot_ready, 1)

            def add_bases():
                dve.wait_ge(wrel_ready, 2 * BASES_FIRST - 1)
                for b in range(BASES_FIRST, N_BASES):
                    base = bases_sb[:, b:b + 1, :].to_broadcast([D, N_REL, D])
                    share = coef_sb[:, :].rearrange("p (r b) -> p r b", b=N_BASES)[:, :, b:b + 1].to_broadcast([D, N_REL, D])
                    own(V.tensor_tensor(w_part_dve[:, :, :], base, share, ALU.mult))
                    V.tensor_tensor(w_rel[:, :, :], w_rel[:, :, :], w_part_dve[:, :, :], ALU.add).then_inc(wrel_ready, 2)
                    dve.wait_ge(wrel_ready, 2 * b + 1)

            dve.wait_ge(ld_edge, 32)
            rank_count(0)
            rank_place(0)
            for b in range(BATCH_BUFS):
                sort_batch(0, b, b)
            dve.wait_ge(sd_ready, 1)
            V.reciprocal(rstd0[:, :, 0], sd[:, :]).then_inc(rstd0_ready, 1)
            batches_alone(nc.vector, 0, sort_batch, BATCH_BUFS, ALONE[0])
            read_sorted(0)
            decode_rows(0)
            decode_keys(0)
            dve.wait_ge(ld_eps, 16)
            own(V.tensor_scalar(eps1[:, :], eps1[:, :], 1.0, None, ALU.add))
            V.tensor_scalar(ident_eps[:, :], ident[:, :], eps1[:, :], None, ALU.mult).then_inc(eps_ready, 1)
            dve.wait_ge(parts_ready, SPLITS)
            rank_count(1)
            for s in (1, 2):
                rank_place(s)
                if s > 1:
                    dve.wait_ge(nhot_used, RING[0] + CHUNKS_BEFORE[s - 1])
                rounds_beside(nc.vector, s - 1, node_hots, sort_batch, add_bases if s == 2 else None)
                if s < 2:
                    read_sorted(s)
                    decode_rows(s)
                    decode_keys(s)
                    rounds_rest(nc.vector, s - 1, node_hots)
                    rank_count(s + 1)

            dve.wait_ge(nhot_used, RING[0] + CHUNKS_BEFORE[2])
            for g, (a0, a1) in enumerate(groups):
                n = min(WIDE, (a1 - a0) * NP)
                if g == LASTB:
                    dve.wait_ge(batch_used, BATCH_BUFS + BATCHES_BEFORE[2] + COLS[2] // BATCH)
                V.tensor_copy(featT[:, a0 * NP:a1 * NP].rearrange("p (b n) -> p b n", n=n),
                              ps[:, g, 0:(a1 - a0) * D].rearrange("p (b c) -> p b c", c=min(2, a1 - a0) * D)[:, :, 0:n]
                              ).then_inc(sums_read, 1)
            read_sorted(2)

            def z_even_copies(tiles):
                for t in tiles:
                    n = 2 * t
                    dve.wait_ge(z_ps, n + 1)
                    if n >= Z_BUFS:
                        dve.wait_ge(z_stored[n % Z_BUFS], 32 * (n // Z_BUFS))
                    V.tensor_copy(z_stage[:, n % Z_BUFS, :], z_half(n)).then_inc(z_even, 1)

            for step in range(NBANK + Z_LAG):
                z_tiles = range(*groups[step - Z_LAG]) if step >= Z_LAG else ()
                z_even_copies(z_tiles[:2])
                if step == NBANK + 2:
                    decode_rows(2)
                if step == NBANK + 3:
                    decode_keys(2)
                g = step - 2
                if 0 <= g < NBANK:
                    a0, a1 = groups[g]
                    dve.wait_ge(sd_ready, g + 2)
                    own(V.reciprocal(rstd[:, a0:a1], sd[:, a0:a1]))
                    V.scalar_tensor_tensor(shift[:, a0:a1], mv[:, a0:a1, 0], -1.0, rstd[:, a0:a1],
                                           ALU.mult, ALU.mult).then_inc(norm_ready, 1)
                g = step - 1
                if 0 <= g < NBANK:
                    a0, a1 = groups[g]
                    y = y_sum[:, 0:a1 - a0, :]
                    dve.wait_ge(y_ps, g + 1)
                    V.tensor_tensor(y, ps[0:NP, 3, 0:(a1 - a0) * D].rearrange("p (t d) -> p t d", d=D),
                                    b2_sb[:, :, :].to_broadcast([NP, a1 - a0, D]), ALU.add).then_inc(y_used, 1)
                    dve.wait_ge(y_used, g + 1)
                    own(V.scalar_tensor_tensor(x_sb[:, a0:a1, :], y, 0.0, x_sb[:, a0:a1, :], ALU.max, ALU.add))
                    mean_var(a0, a1)
                z_even_copies(z_tiles[2:])
            dve.wait_ge(wsT_ps, 1)
            V.tensor_copy(wsT[:, :], ps[:, 7, 0:D]).then_inc(wsT_ready, 1)
            rounds_rest(nc.vector, 2, node_hots)
            dve.wait_ge(nhot_used, RING[0] + sum(CHUNKS))
            for g, (a0, a1) in enumerate(groups):
                V.tensor_tensor(x_sb[:, a0:a1, :], x_sb[:, a0:a1, :],
                                psf[0:NP, a0 * D:a1 * D].rearrange("p (t d) -> p t d", d=D), ALU.add).then_inc(out_ready, 1)

        @block.tensor
        def _(pe):
            T = nc.tensor
            pe.sem_inc(nhot_used, RING[0])
            pe.sem_inc(batch_used, BATCH_BUFS)
            pe.wait_ge(consts_done, 1)

            def zero_bank(b):
                return T.matmul(ps[:, b, :], zeros_h[:, :], iota_h[:, :], start=True, stop=False, skip_group_check=True)

            def rank_sums(l):
                pe.wait_ge(count_ready, l + 1)
                T.matmul(pre_ps, before[0:EP, 0:EP], count[:, :], start=True, stop=True)
                T.matmul(tot_ps, ones[0:EP, :], count[:, :], start=True, stop=True).then_inc(prefix_done, 1)
                pe.wait_ge(bucket_of_ready, l + 1)
                for q in range(-(-CHUNKS[l] // P)):
                    w = min(P, CHUNKS[l] - q * P)
                    last = T.matmul(ps[0:1, 7, q * P:q * P + w], bucket_of[:, q:q + 1], ident[:, 0:w], start=True, stop=True)
                last.then_inc(bucket_row_done, 1)
                pe.wait_ge(bucket_off_ready, l + 1)

            def sort_batch(s, batch, buf):
                pe.wait_ge(batch_ready, batch + (BATCHES_BEFORE[s] + 1))
                for i in range(BATCH):
                    n = batch * BATCH + (COLS_BEFORE[s] + i + 1)
                    for k, c0, c1, where in sort_regions[s]:
                        if k:
                            pe.wait_ge(val_ready, n)
                        val = place_val_b[:, buf, i, :] if k else place_val_a[:, buf, :, i]
                        last = T.matmul(where, val, chunk_hot[:, buf, i, c0:c1], start=False, stop=False,
                                        skip_group_check=True)
                last.then_inc(batch_used, 1)

            def add_up(s, g, r):
                _, offs = nc.values_load_multi_w_load_instructions(
                    bucket_off[s][0:1, bass.ds(r * GROUPS[s] + g, 1), 0:GROUP[s]].rearrange("p g i -> p (g i)"),
                    engines=[mybir.EngineType.PE], min_val=0, max_val=(BUCKETS - 1) * 2 * D,
                    skip_runtime_bounds_check_because="the row is cut to the last bucket")
                pe.wait_ge(got[s][g], r * (16 * GROUP[s]) + 16 * GROUP[s])
                for i in range(GROUP[s]):
                    k = g * GROUP[s] + i
                    pe.wait_ge(nhot_ready, r * RING[s] + (CHUNKS_BEFORE[s] + k + 1))
                    for half in range(2 if s == 2 else 0):
                        last = T.matmul(psf[0:NP, bass.ds(offs[i] + half * D, D)],
                                        node_hot_of[s][:, k % HOTS[s], half * NP:(half + 1) * NP], gathered_of[s][:, k, :],
                                        start=False, stop=False, skip_group_check=True)
                    for part in range(SPLITS if s < 2 else 0):
                        last = T.matmul(psf[:, bass.ds(offs[i], WIDE)], gathered_of[s][:, k, part, :],
                                        node_hot_of[s][:, k % HOTS[s], :], start=False, stop=False, skip_group_check=True)
                    last.then_inc(nhot_used, 1)

            rank_sums(0)
            for b in range(8):
                zero_bank(b)
            batches_alone(nc.tensor, 0, sort_batch, 0, ALONE[0])
            pe.wait_ge(decoded, 1)
            pe.wait_ge(h_ready, 1)
            pe.wait_ge(eps_ready, 1)
            for t in range(TILES):
                c = t // 2 * 2 * D + t % 2 * NP
                T.matmul(psf[:, c:c + NP], h_sb[:, t, :], ident_eps[0:NP, 0:NP], start=False, stop=False, skip_group_check=True)
            rank_sums(1)
            zero_bank(7)
            for s in (1, 2):
                rounds_beside(nc.tensor, s - 1, add_up, sort_batch)
                if s < 2:
                    pe.wait_ge(decoded, s + 1)
                    rounds_rest(nc.tensor, s - 1, add_up)
                    rank_sums(s + 1)
                    zero_bank(7)

            for step in range(NBANK + Z_LAG):
                g = step - 1
                if 0 <= g < NBANK:
                    a0, a1 = groups[g]
                    pe.wait_ge(hid_ready, g + 1)
                    pe.wait_ge(sums_read, 4)
                    if g:
                        pe.wait_ge(y_used, g)
                    for t in range(a0, a1):
                        c = (t - a0) * D
                        last = T.matmul(ps[0:NP, 3, c:c + D], hidT[:, (t - a0) * NP:(t - a0 + 1) * NP], w2_sb[:, :],
                                        start=True, stop=True)
                    last.then_inc(y_ps, 1)
                g = step
                if 0 <= g < NBANK:
                    w = (groups[g][1] - groups[g][0]) * NP
                    pe.wait_ge(sums_read, max(g + 1, 3))
                    pe.wait_ge(ld_w, 80)
                    if g:
                        pe.wait_ge(hid_ready, g)
                    T.matmul(ps[:, 2, 0:w], w1_sb[:, :], featT[:, groups[g][0] * NP:groups[g][1] * NP], start=True,
                             stop=True).then_inc(hid_ps, 1)
                g = step - 3
                if 0 <= g < NBANK:
                    a0, a1 = groups[g]
                    pe.wait_ge(h_ready, g + 2)
                    if g >= 2:
                        pe.wait_ge(h2T_ready, g - 1)
                    for t in range(a0, a1):
                        last = T.transpose(ps[:, g % 2, (t - a0) * NP:(t - a0 + 1) * NP], h_sb[:, t, :], ident[0:NP, 0:NP])
                    last.then_inc(h2T_ps, 1)
                g = step - Z_LAG
                if 0 <= g < NBANK:
                    pe.wait_ge(h2T_ready, g + 1)
                    pe.wait_ge(sums_read, NBANK)
                    pe.wait_ge(sorted_read, 3)
                    pe.wait_ge(wrel_ready, 2 * N_BASES - 1)
                    for t in range(*groups[g]):
                        for half in range(2):
                            if t:
                                pe.wait_ge(z_odd if half else z_even, t)
                            for q in range(2):
                                last = T.matmul(z_half(half)[:, q * BANK:(q + 1) * BANK], h2T[:, t * NP:(t + 1) * NP],
                                                w_rel[:, half * N_REL // 2 + q * BT:half * N_REL // 2 + (q + 1) * BT, :], start=True, stop=True)
                            last.then_inc(z_ps, 1)
            pe.wait_ge(z_even, TILES)
            pe.wait_ge(z_odd, TILES)
            pe.wait_ge(ld_w, 80)
            T.transpose(ps[:, 7, 0:D], ws_sb[:, :], ident[:, :]).then_inc(wsT_ps, 1)
            pe.wait_ge(wsT_ready, 1)
            pe.wait_ge(y_used, NBANK)
            for b in range(NBANK):
                zero_bank(b)
            for t in range(TILES):
                T.matmul(psf[0:NP, t * D:(t + 1) * D], h2T[:, t * NP:(t + 1) * NP], wsT[:, :], start=False, stop=False,
                         skip_group_check=True)
            rounds_rest(nc.tensor, 2, add_up)


_INS = ["x", "src", "dst", "edge_type_16", "L0_gnn_eps", "L0_gnn_W1", "L0_gnn_b1", "L0_gnn_W2", "L0_gnn_b2",
        "L1_gnn_bases", "L1_gnn_coefficients", "L1_gnn_w_self"]


def kernel(**inputs):
    import concourse.bacc as _bacc
    from concourse.bass_utils import run_bass_kernel_spmd as _run

    nc = _bacc.Bacc("TRN2", target_bir_lowering=False, num_devices=1)
    arrays, args = {}, []
    for name in _INS:
        a = np.ascontiguousarray(inputs[name])
        arrays[f"in_{name}"] = a
        args.append(nc.dram_tensor(f"in_{name}", a.shape, mybir.dt.from_np(a.dtype), kind="ExternalInput").ap())
    out = nc.dram_tensor("out", (N_NODES, D), F32, kind="ExternalOutput").ap()
    build(nc, *args, out)
    r = _run(nc, [arrays], core_ids=[0])
    return r.results[0]["out"]
```
